# Optimizing a Trainium2 kernel written in Bass

```python
import numpy as np
import jax
import jax.numpy as jnp

def _softmax(x, axis=-1):
    return jax.nn.softmax(x, axis=axis)

def _gelu(x):
    return jax.nn.gelu(x, approximate=True)

def _silu(x):
    return jax.nn.silu(x)

def _sigmoid(x):
    return jax.nn.sigmoid(x)

def _layernorm(x, axis=-1, eps=1e-05):
    m = jnp.mean(x, axis=axis, keepdims=True)
    v = jnp.var(x, axis=axis, keepdims=True)
    return (x - m) / jnp.sqrt(v + eps)

def _scatter_add(tgt, idx, src, axis=0):
    return tgt.at[idx].add(src)

def _segment_sum(src, seg, n):
    return jax.ops.segment_sum(src, seg, n)
kernel_name = 'mk_recurrent_d2_jaxref_r8_ff32b2'

def setup_inputs(seed: int=0):
    np.random.seed(seed)
    _w = jnp.asarray

    def _L0_attn_setup():
        import jax, jax.numpy as jnp
        import numpy as np
        DIM = 128
        HEADS = 16
        HIDDEN = 512
        B, N = (4, 256)

        def _mlp(x, w1, b1, w2, b2):
            h = jax.nn.gelu(x @ w1 + b1, approximate=False)
            return h @ w2 + b2
        key = jax.random.key(seed)
        ks = jax.random.split(key, 15)
        s_in = 1.0 / np.sqrt(DIM)
        s_hid = 1.0 / np.sqrt(HIDDEN)
        inp = {'x': jax.random.normal(ks[0], (B, N, DIM), dtype=jnp.float32)}
        i = 1
        for name in ('q', 'k', 'v'):
            inp[f'{name}_w1'] = jax.random.normal(ks[i], (DIM, HIDDEN), jnp.float32) * s_in
            i += 1
            inp[f'{name}_b1'] = jax.random.normal(ks[i], (HIDDEN,), jnp.float32) * s_in
            i += 1
            inp[f'{name}_w2'] = jax.random.normal(ks[i], (HIDDEN, DIM), jnp.float32) * s_hid
            i += 1
            inp[f'{name}_b2'] = jax.random.normal(ks[i], (DIM,), jnp.float32) * s_hid
            i += 1
        inp['proj_w'] = jax.random.normal(ks[13], (DIM, DIM), jnp.float32) * s_in
        inp['proj_b'] = jax.random.normal(ks[14], (DIM,), jnp.float32) * s_in
        return inp
    _L0_attn_in = _L0_attn_setup()

    def _L0_ffn_setup():
        import jax, jax.numpy as jnp
        import numpy as np
        LN_EPS = 0.001
        EPS = 1e-05
        QB = 128.0

        def ste_round(x):
            return x + jax.lax.stop_gradient(jnp.round(x) - x)
        key = jax.random.key(seed)
        k1, k2 = jax.random.split(key)
        x = jax.random.normal(k1, (4, 1024, 128), dtype=jnp.float32)
        weight = jax.random.normal(k2, (128, 128), dtype=jnp.float32) * 0.02
        ln_gamma = jnp.ones((128,), dtype=jnp.float32)
        ln_beta = jnp.zeros((128,), dtype=jnp.float32)
        return {'x': x, 'weight': weight, 'ln_gamma': ln_gamma, 'ln_beta': ln_beta}
    _L0_ffn_in = _L0_ffn_setup()

    def _L1_attn_setup():
        import jax, jax.numpy as jnp
        import numpy as np
        B, N, DIM = (4, 128, 128)
        H, DH = (16, 64)
        NUM_MEM = 4
        TOPK = 64
        QK_SCALE = 10.0

        def l2norm(t, eps=1e-12):
            return t / jnp.clip(jnp.linalg.norm(t, axis=-1, keepdims=True), eps)
        key = jax.random.key(seed)
        ks = jax.random.split(key, 12)
        s = 0.02
        inp = {'x': jax.random.normal(ks[0], (B, N, DIM), dtype=jnp.float32), 'Wq': jax.random.normal(ks[1], (DIM, H * DH), dtype=jnp.float32) * s, 'Wk': jax.random.normal(ks[2], (DIM, H * DH), dtype=jnp.float32) * s, 'Wv': jax.random.normal(ks[3], (DIM, H * DH), dtype=jnp.float32) * s, 'W_pre_th': jax.random.normal(ks[4], (H, H), dtype=jnp.float32) * (1.0 / H) ** 0.5, 'W_post_th': jax.random.normal(ks[5], (H, H), dtype=jnp.float32) * (1.0 / H) ** 0.5, 'mem_k': jax.random.normal(ks[6], (H, NUM_MEM, DH), dtype=jnp.float32), 'mem_v': jax.random.normal(ks[7], (H, NUM_MEM, DH), dtype=jnp.float32), 'head_scale_params': jnp.ones((1, H, 1, 1), dtype=jnp.float32), 'Wg': jax.random.normal(ks[8], (DIM, H * DH), dtype=jnp.float32) * s, 'bg': jnp.ones((H * DH,), dtype=jnp.float32), 'Wo': jax.random.normal(ks[9], (H * DH, DIM), dtype=jnp.float32) * s}
        return inp
    _L1_attn_in = _L1_attn_setup()

    def _L1_ffn_setup():
        import jax, jax.numpy as jnp
        import numpy as np
        TOP_K = 2
        key = jax.random.key(seed)
        ks = jax.random.split(key, 6)
        B, S, D, BN, E = (32, 256, 128, 64, 8)
        return {'x': jax.random.normal(ks[0], (B, S, D), dtype=jnp.float32), 'gate_w': jax.random.normal(ks[1], (E, D), dtype=jnp.float32) * 0.02, 'down_w': jax.random.normal(ks[2], (E, BN, D), dtype=jnp.float32) * 0.02, 'down_b': jax.random.normal(ks[3], (E, BN), dtype=jnp.float32) * 0.02, 'up_w': jax.random.normal(ks[4], (E, D, BN), dtype=jnp.float32) * 0.02, 'up_b': jax.random.normal(ks[5], (E, D), dtype=jnp.float32) * 0.02}
    _L1_ffn_in = _L1_ffn_setup()
    _d = {'L0_attn_x': _L0_attn_in['x'], 'L0_attn_q_w1': _L0_attn_in['q_w1'], 'L0_attn_q_b1': _L0_attn_in['q_b1'], 'L0_attn_q_w2': _L0_attn_in['q_w2'], 'L0_attn_q_b2': _L0_attn_in['q_b2'], 'L0_attn_k_w1': _L0_attn_in['k_w1'], 'L0_attn_k_b1': _L0_attn_in['k_b1'], 'L0_attn_k_w2': _L0_attn_in['k_w2'], 'L0_attn_k_b2': _L0_attn_in['k_b2'], 'L0_attn_v_w1': _L0_attn_in['v_w1'], 'L0_attn_v_b1': _L0_attn_in['v_b1'], 'L0_attn_v_w2': _L0_attn_in['v_w2'], 'L0_attn_v_b2': _L0_attn_in['v_b2'], 'L0_attn_proj_w': _L0_attn_in['proj_w'], 'L0_attn_proj_b': _L0_attn_in['proj_b'], 'L0_ffn_weight': _L0_ffn_in['weight'], 'L0_ffn_ln_gamma': _L0_ffn_in['ln_gamma'], 'L0_ffn_ln_beta': _L0_ffn_in['ln_beta'], 'L1_attn_Wq': _L1_attn_in['Wq'], 'L1_attn_Wk': _L1_attn_in['Wk'], 'L1_attn_Wv': _L1_attn_in['Wv'], 'L1_attn_W_pre_th': _L1_attn_in['W_pre_th'], 'L1_attn_W_post_th': _L1_attn_in['W_post_th'], 'L1_attn_mem_k': _L1_attn_in['mem_k'], 'L1_attn_mem_v': _L1_attn_in['mem_v'], 'L1_attn_head_scale_params': _L1_attn_in['head_scale_params'], 'L1_attn_Wg': _L1_attn_in['Wg'], 'L1_attn_bg': _L1_attn_in['bg'], 'L1_attn_Wo': _L1_attn_in['Wo'], 'L1_ffn_gate_w': _L1_ffn_in['gate_w'], 'L1_ffn_down_w': _L1_ffn_in['down_w'], 'L1_ffn_down_b': _L1_ffn_in['down_b'], 'L1_ffn_up_w': _L1_ffn_in['up_w'], 'L1_ffn_up_b': _L1_ffn_in['up_b']}
    _x0 = _d['L0_attn_x']
    _d['L0_attn_x'] = jax.random.normal(jax.random.fold_in(jax.random.key(seed), 1), (2, 1024, 128), dtype=_x0.dtype)
    del _x0
    return _d

def reference(L0_attn_x, L0_attn_q_w1, L0_attn_q_b1, L0_attn_q_w2, L0_attn_q_b2, L0_attn_k_w1, L0_attn_k_b1, L0_attn_k_w2, L0_attn_k_b2, L0_attn_v_w1, L0_attn_v_b1, L0_attn_v_w2, L0_attn_v_b2, L0_attn_proj_w, L0_attn_proj_b, L0_ffn_weight, L0_ffn_ln_gamma, L0_ffn_ln_beta, L1_attn_Wq, L1_attn_Wk, L1_attn_Wv, L1_attn_W_pre_th, L1_attn_W_post_th, L1_attn_mem_k, L1_attn_mem_v, L1_attn_head_scale_params, L1_attn_Wg, L1_attn_bg, L1_attn_Wo, L1_ffn_gate_w, L1_ffn_down_w, L1_ffn_down_b, L1_ffn_up_w, L1_ffn_up_b):

    def _L0_attn_ref(x, q_w1, q_b1, q_w2, q_b2, k_w1, k_b1, k_w2, k_b2, v_w1, v_b1, v_w2, v_b2, proj_w, proj_b):
        import jax, jax.numpy as jnp
        import numpy as np
        DIM = 128
        HEADS = 16
        HIDDEN = 512
        B, N = (4, 256)

        def _mlp(x, w1, b1, w2, b2):
            h = jax.nn.gelu(x @ w1 + b1, approximate=False)
            return h @ w2 + b2
        Bx, Nx, C = x.shape
        hd = C // HEADS
        scale = hd ** (-0.5)

        def split_heads(t):
            return t.reshape(Bx, Nx, HEADS, hd).transpose(0, 2, 1, 3)
        q = split_heads(_mlp(x, q_w1, q_b1, q_w2, q_b2))
        k = split_heads(_mlp(x, k_w1, k_b1, k_w2, k_b2))
        v = split_heads(_mlp(x, v_w1, v_b1, v_w2, v_b2))
        attn = jnp.einsum('bhqd,bhkd->bhqk', q, k) * scale
        attn = jax.nn.softmax(attn, axis=-1)
        out = jnp.einsum('bhqk,bhkd->bhqd', attn, v)
        out = out.transpose(0, 2, 1, 3).reshape(Bx, Nx, C)
        return out @ proj_w + proj_b

    def _L0_ffn_ref(x, weight, ln_gamma, ln_beta):
        import jax, jax.numpy as jnp
        import numpy as np
        LN_EPS = 0.001
        EPS = 1e-05
        QB = 128.0

        def ste_round(x):
            return x + jax.lax.stop_gradient(jnp.round(x) - x)
        mu = jnp.mean(x, axis=-1, keepdims=True)
        var = jnp.var(x, axis=-1, keepdims=True)
        xn = (x - mu) * jax.lax.rsqrt(var + LN_EPS) * ln_gamma + ln_beta
        beta = jnp.mean(jnp.abs(weight))
        w_q = jnp.clip(ste_round(weight / (beta + EPS)), -1.0, 1.0)
        gamma = jnp.max(jnp.abs(xn))
        xq = jnp.clip(xn * QB / gamma, -QB + EPS, QB - EPS)
        y = jnp.einsum('bsd,du->bsu', xq, w_q)
        return y * (gamma * beta / QB)

    def _L1_attn_ref(x, Wq, Wk, Wv, W_pre_th, W_post_th, mem_k, mem_v, head_scale_params, Wg, bg, Wo):
        import jax, jax.numpy as jnp
        import numpy as np
        B, N, DIM = (4, 128, 128)
        H, DH = (16, 64)
        NUM_MEM = 4
        TOPK = 64
        QK_SCALE = 10.0

        def l2norm(t, eps=1e-12):
            return t / jnp.clip(jnp.linalg.norm(t, axis=-1, keepdims=True), eps)
        b, n, _ = x.shape
        q = (x @ Wq).reshape(b, n, H, DH).transpose(0, 2, 1, 3)
        k = (x @ Wk).reshape(b, n, H, DH).transpose(0, 2, 1, 3)
        v = (x @ Wv).reshape(b, n, H, DH).transpose(0, 2, 1, 3)
        mk = jnp.broadcast_to(mem_k[None], (b, H, NUM_MEM, DH))
        mv = jnp.broadcast_to(mem_v[None], (b, H, NUM_MEM, DH))
        k = jnp.concatenate([mk, k], axis=2)
        v = jnp.concatenate([mv, v], axis=2)
        q = l2norm(q)
        k = l2norm(k)
        dots = jnp.einsum('bhid,bhjd->bhij', q, k) * QK_SCALE
        dots = jnp.einsum('hg,bgij->bhij', W_pre_th, dots)
        mask_value = -jnp.finfo(dots.dtype).max
        j = n + NUM_MEM
        col_pos = jnp.arange(j) - NUM_MEM
        causal = jnp.arange(n)[:, None] < col_pos[None, :]
        dots = jnp.where(causal[None, None], mask_value, dots)
        top = jax.lax.top_k(dots, TOPK)[0]
        vk = top[..., -1:]
        dots = jnp.where(dots < vk, mask_value, dots)
        attn = jax.nn.softmax(dots, axis=-1)
        attn = jnp.einsum('hg,bgij->bhij', W_post_th, attn)
        out = jnp.einsum('bhij,bhjd->bhid', attn, v)
        out = out * head_scale_params
        out = out.transpose(0, 2, 1, 3).reshape(b, n, H * DH)
        gates = x @ Wg + bg
        out = out * jax.nn.sigmoid(gates)
        return out @ Wo

    def _L1_ffn_ref(x, gate_w, down_w, down_b, up_w, up_b):
        import jax, jax.numpy as jnp
        import numpy as np
        TOP_K = 2
        pooled = x.mean(axis=1)
        gate = jax.nn.softmax(pooled @ gate_w.T, axis=-1)
        top_w, top_i = jax.lax.top_k(gate, TOP_K)
        top_w = top_w / (top_w.sum(axis=-1, keepdims=True) + 1e-08)
        Wd = down_w[top_i]
        bd = down_b[top_i]
        Wu = up_w[top_i]
        bu = up_b[top_i]
        h = jax.nn.gelu(jnp.einsum('bsd,bkcd->bksc', x, Wd) + bd[:, :, None, :], approximate=False)
        h = h * top_w[:, :, None, None]
        out = jnp.einsum('bksc,bkdc->bsd', h, Wu)
        out = out + (top_w[:, :, None] * bu).sum(axis=1)[:, None, :]
        return out
    x = L0_attn_x
    xn = _layernorm(x, axis=-1)
    s = _L0_attn_ref(xn, L0_attn_q_w1, L0_attn_q_b1, L0_attn_q_w2, L0_attn_q_b2, L0_attn_k_w1, L0_attn_k_b1, L0_attn_k_w2, L0_attn_k_b2, L0_attn_v_w1, L0_attn_v_b1, L0_attn_v_w2, L0_attn_v_b2, L0_attn_proj_w, L0_attn_proj_b)
    g = _silu(_L0_ffn_ref(xn, L0_ffn_weight, L0_ffn_ln_gamma, L0_ffn_ln_beta))
    x = x + s * g
    xn = _layernorm(x, axis=-1)
    s = _L1_attn_ref(xn, L1_attn_Wq, L1_attn_Wk, L1_attn_Wv, L1_attn_W_pre_th, L1_attn_W_post_th, L1_attn_mem_k, L1_attn_mem_v, L1_attn_head_scale_params, L1_attn_Wg, L1_attn_bg, L1_attn_Wo)
    g = _silu(_L1_ffn_ref(xn, L1_ffn_gate_w, L1_ffn_down_w, L1_ffn_down_b, L1_ffn_up_w, L1_ffn_up_b))
    x = x + s * g
    return x

_drawn_inputs = setup_inputs


def setup_inputs(seed=0):
    import zlib

    import numpy as np

    out = dict(_drawn_inputs(seed))
    spreads = {'L0_ffn_ln_gamma': (1.0, 0.6),
     'L0_ffn_ln_beta': (0.0, 0.8),
     'L1_attn_head_scale_params': (1.0, 0.6),
     'L1_attn_bg': (1.0, 0.6)}
    factors = {'L0_attn_q_w1': 8.0,
     'L0_attn_q_b1': 8.0,
     'L0_attn_q_w2': 8.0,
     'L0_attn_q_b2': 8.0,
     'L0_attn_k_w1': 8.0,
     'L0_attn_k_b1': 8.0,
     'L0_attn_k_w2': 8.0,
     'L0_attn_k_b2': 8.0,
     'L0_attn_v_w1': 8.0,
     'L0_attn_v_b1': 8.0,
     'L0_attn_v_b2': 8.0,
     'L0_attn_proj_w': 2.85,
     'L0_attn_proj_b': 8.0,
     'L1_attn_Wq': 8.0,
     'L1_attn_Wk': 8.0,
     'L1_attn_Wv': 8.0,
     'L1_attn_W_pre_th': 8.0,
     'L1_attn_W_post_th': 8.0,
     'L1_attn_mem_k': 8.0,
     'L1_attn_mem_v': 8.0,
     'L1_attn_Wg': 8.0,
     'L1_attn_Wo': 8.0,
     'L1_ffn_gate_w': 8.0,
     'L1_ffn_down_w': 8.0,
     'L1_ffn_down_b': 8.0,
     'L1_ffn_up_w': 8.0,
     'L1_ffn_up_b': 8.0}
    for name, (base, spread) in spreads.items():
        noise = np.random.default_rng([zlib.crc32(name.encode()), seed]).standard_normal(out[name].shape)
        drawn = base * np.exp(spread * noise) if base else spread * noise
        out[name] = jnp.asarray(drawn.astype(out[name].dtype))
    for name, factor in factors.items():
        out[name] = (out[name] * factor).astype(out[name].dtype)
    return out
```

```python
from contextlib import ExitStack

import concourse.bass as bass
from concourse import mybir

ALU = mybir.AluOpType
ACT = mybir.ActivationFunctionType
F32 = mybir.dt.float32
BF16 = mybir.dt.bfloat16
I32 = mybir.dt.int32
AX_X = mybir.AxisListType.X
RMAX = bass.bass_isa.ReduceOp.max
RADD = bass.bass_isa.ReduceOp.add

P = 128
BIG = 3.4028234663852886e38
ROUND = 12582912.0
QB = 128.0


def program(nc, A, out, debug=None):
    B, N, D = A["L0_attn_x"].shape
    HID = A["L0_attn_q_w1"].shape[1]
    HT = HID // P
    H = A["L1_attn_W_pre_th"].shape[0]
    DH0 = D // H
    HW = A["L1_attn_Wq"].shape[1]
    DH1 = HW // H
    MEM = A["L1_attn_mem_k"].shape[1]
    E, BN, _ = A["L1_ffn_down_w"].shape
    NT = N // P
    T = B * NT
    PAIRS = H // 2
    IL = P // H
    SPLITS = 3
    KR = SPLITS * SPLITS * DH0
    KW = MEM + N

    with ExitStack() as top:
        def sb(name, shape, dt=F32, ctx=top):
            return ctx.enter_context(nc.sbuf_tensor(name, shape, dt))

        def ps(name, shape, ctx, dt=F32):
            return ctx.enter_context(nc.psum_tensor(name, shape, dt))

        def sem(name, ctx=top):
            return ctx.enter_context(nc.semaphore(name))

        ident = sb("ident", [P, P])
        d8 = sb("d8", [P, IL])
        d32 = sb("d32", [P, 32])
        headones = sb("headones", [P, P])
        ones1 = sb("ones1", [P, P])
        slide = sb("slide", [P, 2 * DH1 - IL])
        kron_pre = sb("kron_pre", [P, H, IL])
        kron_post = sb("kron_post", [P, H, IL])

        xnT_dram = nc.dram_tensor("xnT_dram", [P, T * P], F32, kind="Internal").ap()
        g0_dram = nc.dram_tensor("g0_dram", [P, T, D], F32, kind="Internal").ap()

        with ExitStack() as ctx:
            x_all = sb("x_all", [P, T, D], ctx=ctx)
            xnT_all = sb("xnT_all", [P, T * P], ctx=ctx)
            g0_all = sb("g0_all", [P, T, D], ctx=ctx)
            wq8 = sb("wq8", [P, D], ctx=ctx)
            fw = sb("fw", [P, D], ctx=ctx)
            lng = sb("lng", [P, D], ctx=ctx)
            lnb = sb("lnb", [P, D], ctx=ctx)
            wpre = sb("wpre", [P, H], ctx=ctx)
            wpost = sb("wpost", [P, H], ctx=ctx)
            stats = sb("stats", [P, T, 6], ctx=ctx)
            mv = sb("mv", [P, T, 2], ctx=ctx)
            stats2 = sb("stats2", [P, T, 6], ctx=ctx)
            mv2 = sb("mv2", [P, T, 2], ctx=ctx)
            std = sb("std", [P, 2, T], ctx=ctx)
            rstd = sb("rstd", [P, 2, T], ctx=ctx)
            xn = sb("xn", [P, T, D], ctx=ctx)
            xq = sb("xq", [P, T, D], ctx=ctx)
            scratch = sb("scratch", [P, T, D], ctx=ctx)
            xqT = sb("xqT", [P, T * P], ctx=ctx)
            amax = sb("amax", [P, 1], ctx=ctx)
            gmax = sb("gmax", [P, 1], ctx=ctx)
            asum = sb("asum", [P, 1], ctx=ctx)
            gsum = sb("gsum", [P, 1], ctx=ctx)
            cols = sb("cols", [P, 8], ctx=ctx)
            icol = sb("icol", [P, 2 * DH1 - IL], I32, ctx=ctx)
            fcol = sb("fcol", [P, 2 * DH1 - IL], ctx=ctx)
            irow = sb("irow", [P, IL], I32, ctx=ctx)
            frow = sb("frow", [P, IL], ctx=ctx)
            il = sb("il", [P, 1], ctx=ctx)
            ps_t = ps("ps_t", [P, 4, 512], ctx)
            ps_y = ps("ps_y", [P, 4, 512], ctx)

            x_in = sem("x_in", ctx)
            w_in = sem("w_in", ctx)
            consts = sem("consts", ctx)
            reduced = sem("reduced", ctx)
            dve_step = sem("dve_step", ctx)
            var_ready = sem("var_ready", ctx)
            std_ready = sem("std_ready", ctx)
            xn_ready = sem("xn_ready", ctx)
            xn2_ready = sem("xn2_ready", ctx)
            abs_ready = sem("abs_ready", ctx)
            wabs_ready = sem("wabs_ready", ctx)
            sums_ready = sem("sums_ready", ctx)
            xq_ready = sem("xq_ready", ctx)
            wq_ready = sem("wq_ready", ctx)
            turned = sem("turned", ctx)
            xnT_done = sem("xnT_done", ctx)
            xqT_done = sem("xqT_done", ctx)
            y_ready = sem("y_ready", ctx)
            gate_done = sem("gate_done", ctx)
            stored = sem("stored", ctx)

            block = ctx.enter_context(nc.Block())

            @block.sync
            def _(sp):
                xr = A["L0_attn_x"].rearrange("b (t p) d -> p (b t) d", p=P)
                sp.dma_start(x_all[:], xr).then_inc(x_in, 16)
                sp.dma_start(fw[:], A["L0_ffn_weight"]).then_inc(w_in, 16)
                sp.dma_start(lng[:], A["L0_ffn_ln_gamma"].partition_broadcast(P)).then_inc(w_in, 16)
                sp.dma_start(lnb[:], A["L0_ffn_ln_beta"].partition_broadcast(P)).then_inc(w_in, 16)
                with nc.allow_non_contiguous_dma("2048 single weights, once"):
                    for i in range(IL):
                        for w, t in (("L1_attn_W_pre_th", wpre), ("L1_attn_W_post_th", wpost)):
                            sp.dma_start(t[i:P:IL, :], A[w].rearrange("h g -> g h")).then_inc(w_in, 16)

                sp.wait_ge(xnT_done, T // 4)
                sp.dma_start(xnT_dram, xnT_all[:]).then_inc(stored, 16)
                sp.wait_ge(gate_done, T // 4)
                sp.dma_start(g0_dram, g0_all[:]).then_inc(stored, 16)
                sp.wait_ge(stored, 32)

            WEIGHTS_IN = 16 * (3 + 2 * IL)

            @block.gpsimd
            def _(pool):
                nc.gpsimd.memset(ident[:], 0.0).then_inc(consts, 1)
                pool.wait_ge(consts, 1)
                nc.gpsimd.affine_select(out=ident[:], in_=ident[:], compare_op=ALU.not_equal, fill=1.0, base=0,
                                        pattern=[[-1, P]], channel_multiplier=1).then_inc(consts, 1)
                nc.gpsimd.iota(icol[:], [[1, 2 * DH1 - IL]], base=IL - DH1, channel_multiplier=0).then_inc(consts, 1)
                nc.gpsimd.iota(irow[:], [[1, IL]], base=0, channel_multiplier=0).then_inc(consts, 1)
                nc.gpsimd.memset(ones1[:], 1.0).then_inc(consts, 1)
                pool.wait_ge(sums_ready, 1)
                nc.gpsimd.partition_all_reduce(gsum[:], asum[:], P, RADD).then_inc(reduced, 1)
                pool.wait_ge(sums_ready, 2)
                nc.gpsimd.partition_all_reduce(gmax[:], amax[:], P, RMAX).then_inc(reduced, 1)

            @block.scalar
            def _(act):
                act.wait_ge(w_in, WEIGHTS_IN)
                nc.scalar.activation(wq8[:], fw[:], ACT.Abs).then_inc(wabs_ready, 1)
                for k in range(2):
                    act.wait_ge(var_ready, k + 1)
                    nc.scalar.activation(std[:, k, :], (mv, mv2)[k][:, :, 1], ACT.Sqrt).then_inc(std_ready, 1)
                for q in range(T // 4):
                    act.wait_ge(turned, q + 1)
                    nc.scalar.copy(xnT_all[:, q * 512:(q + 1) * 512], ps_t[:, q, :]).then_inc(xnT_done, 1)
                act.wait_ge(xn2_ready, 1)
                nc.scalar.activation(scratch[:], xq[:], ACT.Abs).then_inc(abs_ready, 1)
                for q in range(T // 4):
                    act.wait_ge(turned, T // 4 + q + 1)
                    nc.scalar.copy(xqT[:, q * 512:(q + 1) * 512], ps_t[:, q, :]).then_inc(xqT_done, 1)
                act.wait_ge(wq_ready, 1)
                for q in range(T // 4):
                    act.wait_ge(y_ready, q + 1)
                    nc.scalar.activation(g0_all[:, 4 * q:4 * q + 4, :], ps_y[:, q, :], ACT.Silu,
                                         scale=cols[:, 4:5]).then_inc(gate_done, 1)

            @block.vector
            def _(dve):
                steps = [0]

                def link(ins):
                    steps[0] += 1
                    ins.then_inc(dve_step, 1)
                    dve.wait_ge(dve_step, steps[0])

                nc.vector.memset(headones[:], 0.0).then_inc(dve_step, 1)
                steps[0] = 1
                dve.wait_ge(dve_step, 1)
                nc.vector.memset(headones[0:DH1, 0:DH1], 1.0).then_inc(dve_step, 1)
                nc.vector.memset(headones[DH1:P, DH1:P], 1.0).then_inc(dve_step, 1)
                steps[0] = 3
                dve.wait_ge(x_in, 16)
                for t in range(T):
                    ins = nc.vector.bn_stats(stats[:, t, :], x_all[:, t, :])
                link(ins)
                for t in range(T):
                    ins = nc.vector.bn_aggr(mv[:, t, :], stats[:, t, :])
                link(ins)
                nc.vector.tensor_scalar_add(mv[:, :, 1], mv[:, :, 1], 1e-5).then_inc(var_ready, 1)
                dve.wait_ge(wabs_ready, 1)
                nc.vector.reduce_sum(asum[:], wq8[:], AX_X).then_inc(sums_ready, 1)
                dve.wait_ge(consts, 5)
                link(nc.vector.reduce_sum(d8[:], ident[:].rearrange("p (g i) -> p i g", i=IL), AX_X))
                link(nc.vector.reduce_sum(d32[:], ident[:].rearrange("p (g i) -> p i g", i=32), AX_X))
                link(nc.vector.tensor_copy(frow[:], irow[:]))
                link(nc.vector.tensor_copy(fcol[:], icol[:]))
                link(nc.vector.tensor_tensor(frow[:], frow[:], d8[:], ALU.mult))
                link(nc.vector.reduce_sum(il[:], frow[:], AX_X))
                link(nc.vector.tensor_scalar(slide[:], fcol[:], il[:, 0:1], -BIG, ALU.is_gt, ALU.mult))
                dve.wait_ge(w_in, WEIGHTS_IN)
                for src, kron in ((wpre, kron_pre), (wpost, kron_post)):
                    link(nc.vector.tensor_tensor(kron[:], src[:].unsqueeze(2).to_broadcast([P, H, IL]),
                                                 d8[:].unsqueeze(1).to_broadcast([P, H, IL]), ALU.mult))
                dve.wait_ge(std_ready, 1)
                link(nc.vector.reciprocal(rstd[:, 0, :], std[:, 0, :]))
                for t in range(T):
                    ins = nc.vector.tensor_scalar(xn[:, t, :], x_all[:, t, :], mv[:, t, 0:1], rstd[:, 0, t:t + 1],
                                                  ALU.subtract, ALU.mult)
                    if t % 4 == 3:
                        ins.then_inc(xn_ready, 1)
                dve.wait_ge(xn_ready, T // 4)
                for t in range(T):
                    ins = nc.vector.bn_stats(stats2[:, t, :], xn[:, t, :])
                link(ins)
                for t in range(T):
                    ins = nc.vector.bn_aggr(mv2[:, t, :], stats2[:, t, :])
                link(ins)
                nc.vector.tensor_scalar_add(mv2[:, :, 1], mv2[:, :, 1], 1e-3).then_inc(var_ready, 1)
                dve.wait_ge(std_ready, 2)
                link(nc.vector.reciprocal(rstd[:, 1, :], std[:, 1, :]))
                for t in range(T):
                    ins = nc.vector.tensor_scalar(xq[:, t, :], xn[:, t, :], mv2[:, t, 0:1], rstd[:, 1, t:t + 1],
                                                  ALU.subtract, ALU.mult)
                link(ins)
                link(nc.vector.tensor_tensor(xq[:], xq[:], lng[:].unsqueeze(1).to_broadcast([P, T, D]), ALU.mult))
                nc.vector.tensor_tensor(xq[:], xq[:], lnb[:].unsqueeze(1).to_broadcast([P, T, D]),
                                        ALU.add).then_inc(xn2_ready, 1)
                dve.wait_ge(abs_ready, 1)
                nc.vector.reduce_max(amax[:], scratch[:].rearrange("p t d -> p (t d)"), AX_X).then_inc(sums_ready, 1)
                dve.wait_ge(reduced, 1)
                link(nc.vector.tensor_scalar(cols[:, 0:1], gsum[:], 1.0 / (D * D), None, ALU.mult))
                link(nc.vector.tensor_scalar(cols[:, 1:2], cols[:, 0:1], 1e-5, None, ALU.add))
                link(nc.vector.reciprocal(cols[:, 2:3], cols[:, 1:2]))
                link(nc.vector.tensor_scalar(wq8[:], fw[:], cols[:, 2:3], ROUND, ALU.mult, ALU.add))
                link(nc.vector.tensor_scalar(wq8[:], wq8[:], ROUND, 1.0, ALU.subtract, ALU.min))
                link(nc.vector.tensor_scalar(wq8[:], wq8[:], -1.0, None, ALU.max))
                dve.wait_ge(reduced, 2)
                link(nc.vector.reciprocal(cols[:, 3:4], gmax[:]))
                link(nc.vector.tensor_scalar(cols[:, 3:4], cols[:, 3:4], QB, None, ALU.mult))
                link(nc.vector.tensor_scalar(xq[:], xq[:], cols[:, 3:4], QB - 1e-5, ALU.mult, ALU.min))
                nc.vector.tensor_scalar(xq[:], xq[:], -QB + 1e-5, None, ALU.max).then_inc(xq_ready, 1)
                link(nc.vector.tensor_tensor(cols[:, 4:5], gmax[:], cols[:, 0:1], ALU.mult))
                nc.vector.tensor_scalar(cols[:, 4:5], cols[:, 4:5], 1.0 / QB, None, ALU.mult).then_inc(wq_ready, 1)

            @block.tensor
            def _(pe):
                pe.wait_ge(consts, 2)
                for q in range(T // 4):
                    pe.wait_ge(xn_ready, q + 1)
                    for t in range(4 * q, 4 * q + 4):
                        mm = nc.tensor.transpose(ps_t[:, q, (t % 4) * P:(t % 4 + 1) * P], xn[:, t, :], ident[:])
                    mm.then_inc(turned, 1)
                pe.wait_ge(xq_ready, 1)
                for q in range(T // 4):
                    pe.wait_ge(xnT_done, q + 1)
                    for t in range(4 * q, 4 * q + 4):
                        mm = nc.tensor.transpose(ps_t[:, q, (t % 4) * P:(t % 4 + 1) * P], xq[:, t, :], ident[:])
                    mm.then_inc(turned, 1)
                pe.wait_ge(wq_ready, 1)
                for q in range(T // 4):
                    pe.wait_ge(xqT_done, q + 1)
                    for t in range(4 * q, 4 * q + 4):
                        mm = nc.tensor.matmul(ps_y[:, q, (t % 4) * P:(t % 4 + 1) * P], xqT[:, t * P:(t + 1) * P],
                                              wq8[:], start=True, stop=True)
                    mm.then_inc(y_ready, 1)

        qk_parts = nc.dram_tensor("qk_parts", [2, SPLITS, P, N], BF16, kind="Internal").ap()

        def fresh(ctx, *names):
            sems = [sem(n, ctx) for n in names]
            with nc.Block() as reset:
                @reset.gpsimd
                def _(pool):
                    for s in sems:
                        pool.sem_clear(s)
            return sems

        with nc.Fori(0, B) as batch, ExitStack() as per_batch:
            ao = sb("ao", [P, NT, D], ctx=per_batch)

            with ExitStack() as layer0:
                va = sb("va", [P, NT, H, DH0 + 1], ctx=layer0)
                qsp = sb("qsp", [KR + 2, H, N], BF16, ctx=layer0)
                ksp = sb("ksp", [KR + 2, H, N], BF16, ctx=layer0)

                with ExitStack() as ctx:
                    xnT0 = sb("xnT0", [P, N], ctx=ctx)
                    w1 = [sb(f"{m}_w1", [P, HID], ctx=ctx) for m in "qkv"]
                    w2 = [sb(f"{m}_w2", [P, HT, D], ctx=ctx) for m in "qkv"]
                    b1 = sb("b1", [P, 3, HT], ctx=ctx)
                    b2 = sb("b2", [P, 2], ctx=ctx)
                    b2v = sb("b2v", [P, D], ctx=ctx)
                    hid = sb("hid", [P, 2, HT, 512], ctx=ctx)
                    rest = sb("rest", [P, 3, 512], ctx=ctx)
                    parts = sb("parts", [P, 2, SPLITS, N], BF16, ctx=ctx)
                    ps_h = ps("ps_h", [P, HT, 512], ctx)
                    ps_o = ps("ps_o", [P, 2, 512], ctx)
                    (weights_in, ones_set, hid_ready, gelu_done, out_ready, out_read, parts_stored, spread_in,
                     step) = fresh(ctx, "weights_in", "ones_set", "hid_ready", "gelu_done", "out_ready", "out_read",
                                   "parts_stored", "spread_in", "mlp_step")
                    LOADS = 13
                    STEPS = [(m, c) for m in range(3) for c in range(N // 512)]
                    SCALE = float(DH0) ** -0.5

                    with nc.Block() as block:
                        @block.sync
                        def _(sp):
                            sp.dma_start(xnT0[:], xnT_dram[:, bass.ds(batch * N, N)]).then_inc(weights_in, 16)
                            with nc.allow_non_contiguous_dma("biases, one value a partition"):
                                for m, name in enumerate("qkv"):
                                    sp.dma_start(w1[m][:], A[f"L0_attn_{name}_w1"]).then_inc(weights_in, 16)
                                    sp.dma_start(w2[m][:], A[f"L0_attn_{name}_w2"].rearrange("(i p) d -> p i d", p=P)
                                                 ).then_inc(weights_in, 16)
                                    sp.dma_start(b1[:, m, :], A[f"L0_attn_{name}_b1"].rearrange("(i p) -> p i", p=P)
                                                 ).then_inc(weights_in, 16)
                                for m, name in enumerate("qk"):
                                    sp.dma_start(b2[:, m:m + 1], A[f"L0_attn_{name}_b2"].rearrange("(p o) -> p o", o=1)
                                                 ).then_inc(weights_in, 16)
                                sp.dma_start(b2v[:], A["L0_attn_v_b2"].partition_broadcast(P)).then_inc(weights_in, 16)
                            for m in range(2):
                                sp.wait_ge(out_read, 2 * (m + 1))
                                sp.dma_start(qk_parts[m].rearrange("j p n -> p j n"), parts[:, m]
                                             ).then_inc(parts_stored, 16)
                            sp.wait_ge(ones_set, 2)
                            for m, dst in enumerate((qsp, ksp)):
                                sp.wait_ge(parts_stored, 16 * 2)
                                for i in range(SPLITS):
                                    for j in range(SPLITS):
                                        r = (SPLITS * i + j) * DH0
                                        src = qk_parts[m, (i, j)[m]].rearrange("(h d) n -> d h n", d=DH0)
                                        sp.dma_start(dst[r:r + DH0], src).then_inc(spread_in, 16)
                            sp.wait_ge(spread_in, 16 * 2 * SPLITS * SPLITS)

                        @block.gpsimd
                        def _(pool):
                            nc.gpsimd.memset(va[:, :, :, DH0:DH0 + 1], 1.0).then_inc(ones_set, 1)
                            pool.wait_ge(ones_set, 1)
                            nc.gpsimd.memset(ksp[KR - DH0:KR + 2], 1.0).then_inc(ones_set, 1)

                        @block.tensor
                        def _(pe):
                            pe.wait_ge(weights_in, 16 * LOADS)
                            for s in range(len(STEPS) + 1):
                                if s < len(STEPS):
                                    m, c = STEPS[s]
                                    for i in range(HT):
                                        if s >= 1:
                                            pe.wait_ge(gelu_done, HT * (s - 1) + i + 1)
                                        nc.tensor.matmul(ps_h[:, i, :], w1[m][:, i * P:(i + 1) * P],
                                                         xnT0[:, c * 512:(c + 1) * 512],
                                                         start=True, stop=True).then_inc(hid_ready, 1)
                                if s >= 1:
                                    m, c = STEPS[s - 1]
                                    pe.wait_ge(gelu_done, HT * s)
                                    if s >= 3:
                                        pe.wait_ge(out_read, s - 2)
                                    o = ps_o[:, (s - 1) % 2, :]
                                    h = hid[:, (s - 1) % 2]
                                    if m < 2:
                                        for i in range(HT):
                                            mm = nc.tensor.matmul(o, w2[m][:, i, :], h[:, i, :],
                                                                  start=(i == 0), stop=(i == HT - 1))
                                    else:
                                        for t in range(4):
                                            for i in range(HT):
                                                mm = nc.tensor.matmul(o[:, t * P:(t + 1) * P], h[:, i, t * P:(t + 1) * P],
                                                                      w2[m][:, i, :], start=(i == 0), stop=(i == HT - 1))
                                    mm.then_inc(out_ready, 1)

                        @block.scalar
                        def _(act):
                            for s, (m, c) in enumerate(STEPS):
                                if s >= 2:
                                    act.wait_ge(out_ready, s - 1)
                                for i in range(HT):
                                    act.wait_ge(hid_ready, HT * s + i + 1)
                                    nc.scalar.activation(hid[:, s % 2, i, :], ps_h[:, i, :], ACT.Gelu,
                                                         bias=b1[:, m, i:i + 1]).then_inc(gelu_done, 1)

                        @block.vector
                        def _(dve):
                            n = [0]

                            def link(ins):
                                n[0] += 1
                                ins.then_inc(step, 1)
                                dve.wait_ge(step, n[0])

                            for s, (m, c) in enumerate(STEPS):
                                dve.wait_ge(out_ready, s + 1)
                                o = ps_o[:, s % 2, :]
                                if m < 2:
                                    link(nc.vector.tensor_scalar(rest[:, 0], o, b2[:, m:m + 1], (SCALE, 1.0)[m],
                                                                 ALU.add, ALU.mult))
                                    for j in range(SPLITS):
                                        part = parts[:, m, j, c * 512:(c + 1) * 512]
                                        ins = nc.vector.tensor_copy(part, rest[:, j])
                                        if j < SPLITS - 1:
                                            link(ins)
                                            link(nc.vector.tensor_tensor(rest[:, j + 1], rest[:, j], part, ALU.subtract))
                                    ins.then_inc(out_read, 1)
                                else:
                                    nc.vector.tensor_tensor(
                                        va[:, 4 * c:4 * c + 4, :, 0:DH0], o.rearrange("p (t h d) -> p t h d", t=4, d=DH0),
                                        b2v[:].rearrange("p (h d) -> p h d", d=DH0).unsqueeze(1)
                                        .to_broadcast([P, 4, H, DH0]), ALU.add).then_inc(out_read, 1)

                with ExitStack() as ctx:
                    va_cur = sb("va_cur", [P, NT, 32], ctx=ctx)
                    pt = sb("pt", [P, NT, 512], ctx=ctx)
                    mx = sb("mx", [P, NT], ctx=ctx)
                    nm = sb("nm", [NT, 2, P], BF16, ctx=ctx)
                    nm32 = sb("nm32", [NT, P], ctx=ctx)
                    ot_sb = sb("ot_sb", [P, 512], ctx=ctx)
                    rec = sb("rec", [P, 4], ctx=ctx)
                    sm = ps("sm", [P, 2, N], ctx)
                    st = ps("st", [P, 2, 512], ctx)
                    ot = ps("ot", [P, 512], ctx)
                    misc = ps("misc", [P, 512], ctx)
                    (sm_ready, sm_free, st_ready, st_free, maxes_ready, turn_ready, misc_free, negmax_part, negmax_ready, negmax_in,
                     va_ready, pv_ready, ot_copied, nat_ready, rec_ready, zeroed, gate) = fresh(
                        ctx, "sm_ready", "sm_free", "st_ready", "st_free", "maxes_ready", "turn_ready", "misc_free",
                        "negmax_part", "negmax_ready", "negmax_in", "va_ready", "pv_ready", "ot_copied", "nat_ready",
                        "rec_ready", "zeroed", "gate")
                    QC = N // 512

                    with nc.Block() as block:
                        @block.sync
                        def _(sp):
                            def negmax(h):
                                sp.wait_ge(negmax_ready, h + 1)
                                for r in range(2):
                                    sp.dma_start(qsp[KR + r:KR + r + 1, bass.ds(h, 1), :]
                                                 .rearrange("r o (t q) -> r (o t) q", q=P),
                                                 nm[:, r]).then_inc(negmax_in, 16)

                            negmax(0)
                            with sp.Fori(0, H - 1) as h:
                                negmax(h + 1)

                        @block.gpsimd
                        def _(pool):
                            nc.gpsimd.memset(va_cur[:], 0.0).then_inc(zeroed, 1)
                            pool.wait_ge(zeroed, 1)
                            with pool.Fori(0, H) as h:
                                pool.wait_ge(pv_ready, h * (2 * QC))
                                pool.sem_inc(gate, 1)
                                nc.gpsimd.tensor_copy(va_cur[:, :, 0:DH0 + 1],
                                                      va[:, :, bass.ds(h, 1), :]).then_inc(va_ready, 1)

                        @block.tensor
                        def _(pe):
                            def score_max(h, qt):
                                pe.wait_ge(sm_free, h * NT + qt + 1)
                                for kc in range(QC):
                                    mm = nc.tensor.matmul(sm[:, qt % 2, kc * 512:(kc + 1) * 512],
                                                          qsp[0:KR, bass.ds(h, 1), qt * P:(qt + 1) * P],
                                                          ksp[0:KR, bass.ds(h, 1), kc * 512:(kc + 1) * 512],
                                                          start=True, stop=True)
                                mm.then_inc(sm_ready, 1)

                            def turn_max(h, use):
                                pe.wait_ge(maxes_ready, h + 1)
                                pe.wait_ge(misc_free, use)
                                nc.tensor.transpose(misc[0:NT, 0:P], mx[:], ident[:]).then_inc(turn_ready, 1)

                            def score(h, qc, kt):
                                pe.wait_ge(st_free, (h * QC + qc) * NT + kt + 1)
                                if qc == 0 and kt == 0:
                                    pe.wait_ge(negmax_in, 32 * (h + 1))
                                nc.tensor.matmul(st[:, kt % 2, :], ksp[:, bass.ds(h, 1), kt * P:(kt + 1) * P],
                                                 qsp[:, bass.ds(h, 1), qc * 512:(qc + 1) * 512],
                                                 start=True, stop=True).then_inc(st_ready, 1)

                            def weigh(h, qc, half):
                                if half == 0:
                                    if qc == 0:
                                        pe.wait_ge(va_ready, h + 1)
                                    pe.wait_ge(ot_copied, h * QC + qc)
                                pe.wait_ge(st_free, 2 + (h * QC + qc) * NT + 4 * half + 4)
                                for c in range(4):
                                    mm = nc.tensor.matmul(ot[32 * c:32 * c + 32, :], va_cur[:, 4 * half + c, :],
                                                          pt[:, 4 * half + c, :], start=(half == 0), stop=(half == 1))
                                mm.then_inc(pv_ready, 1)

                            def natural(h, qc, use):
                                pe.wait_ge(ot_copied, h * QC + qc + 1)
                                pe.wait_ge(misc_free, use)
                                for j in range(4):
                                    mm = nc.tensor.matmul(misc[:, 16 * j:16 * j + DH0 + 1], ot_sb[:, j * P:(j + 1) * P],
                                                          d32[:, 0:DH0 + 1], start=True, stop=True)
                                mm.then_inc(nat_ready, 1)

                            def head(h, ahead):
                                for qc in range(QC):
                                    for kt in range(NT):
                                        score(h, qc, kt)
                                        if ahead and kt % 2 == 1:
                                            score_max(h + 1, qc * 4 + kt // 2)
                                        if qc == 1 and kt == 1:
                                            weigh(h, 0, 1)
                                        if qc == 1 and kt == 3:
                                            natural(h, 0, 3 * h + 2)
                                        if kt == 5:
                                            weigh(h, qc, 0)
                                if ahead:
                                    turn_max(h + 1, 3 * h + 3)
                                weigh(h, 1, 1)
                                natural(h, 1, 3 * h + 3 + ahead)

                            for qt in range(NT):
                                score_max(0, qt)
                            turn_max(0, 1)
                            with pe.Fori(0, H - 1) as h:
                                head(h, 1)
                            head(H - 1, 0)

                        @block.scalar
                        def _(act):
                            def exps(u, first):
                                for kt in range(NT):
                                    act.wait_ge(st_ready, u * NT + kt + 1)
                                    if kt % 4 == 0 and not first:
                                        act.wait_ge(pv_ready, u * 2 - 1 + kt // 4)
                                    nc.scalar.activation(pt[:, kt, :], st[:, kt % 2, :], ACT.Exp).then_inc(st_free, 1)

                            exps(0, True)
                            with act.Fori(1, H * QC) as u:
                                exps(u, False)

                        @block.vector
                        def _(dve):
                            dve.sem_inc(sm_free, 2)
                            dve.sem_inc(st_free, 2)
                            dve.sem_inc(misc_free, 1)

                            def row_max(h, qt):
                                dve.wait_ge(sm_ready, h * NT + qt + 1)
                                ins = nc.vector.reduce_max(mx[:, qt:qt + 1], sm[:, qt % 2, :], AX_X)
                                ins.then_inc(sm_free, 1)

                            def negate(h):
                                dve.wait_ge(turn_ready, h + 1)
                                nc.vector.tensor_scalar(nm32[:], misc[0:NT, 0:P], -1.0, None,
                                                        ALU.mult).then_inc(negmax_part, 1)
                                dve.wait_ge(negmax_part, 2 * h + 1)
                                dve.sem_inc(misc_free, 1)
                                nc.vector.tensor_copy(nm[:, 0], nm32[:]).then_inc(negmax_part, 1)
                                dve.wait_ge(negmax_part, 2 * h + 2)
                                nc.vector.tensor_tensor(nm[:, 1], nm32[:], nm[:, 0],
                                                        ALU.subtract).then_inc(negmax_ready, 1)

                            def copy_sums(h, qc):
                                dve.wait_ge(pv_ready, (h * QC + qc) * 2 + 2)
                                nc.vector.tensor_copy(ot_sb[:], ot[:]).then_inc(ot_copied, 1)

                            def normalise(h, qc):
                                dve.wait_ge(nat_ready, h * QC + qc + 1)
                                m = misc[:, 0:64].rearrange("p (j c) -> p j c", c=16)
                                nc.vector.reciprocal(rec[:], m[:, :, DH0]).then_inc(rec_ready, 1)
                                dve.wait_ge(rec_ready, h * QC + qc + 1)
                                nc.vector.tensor_tensor(ao[:, 4 * qc:4 * qc + 4, bass.ds(h * DH0, DH0)], m[:, :, 0:DH0],
                                                        rec[:].unsqueeze(2).to_broadcast([P, 4, DH0]),
                                                        ALU.mult).then_inc(misc_free, 1)

                            def head(h, ahead):
                                for qt in range(NT):
                                    if ahead:
                                        row_max(h + 1, qt)
                                    if qt == 4:
                                        copy_sums(h, 0)
                                    if qt == 5:
                                        normalise(h, 0)
                                if ahead:
                                    dve.wait_ge(sm_free, 2 + (h + 1) * NT + NT)
                                    dve.sem_inc(maxes_ready, 1)
                                    negate(h + 1)
                                copy_sums(h, 1)
                                normalise(h, 1)

                            for qt in range(NT):
                                row_max(0, qt)
                            dve.wait_ge(sm_free, 2 + NT)
                            dve.sem_inc(maxes_ready, 1)
                            negate(0)
                            with dve.Fori(0, H - 1) as h:
                                head(h, 1)
                            head(H - 1, 0)
            xb = sb("xb", [P, NT, D], ctx=per_batch)
            g1 = sb("g1", [P, NT, D], ctx=per_batch)
            xnT = sb("xnT", [P, KW], ctx=per_batch)
            qT = sb("qT", [P, PAIRS, N], ctx=per_batch)
            kT = sb("kT", [P, PAIRS, KW], ctx=per_batch)
            VB = 1 + (N - DH1 + P - 1) // P
            vn = sb("vn", [P, VB, HW], ctx=per_batch)
            rows_of = [MEM + DH1] + [min(P, N - DH1 - P * k) for k in range(VB - 1)]
            first_of = [0] + [MEM + DH1 + P * k for k in range(VB - 1)]

            with ExitStack() as ctx:
                pw = sb("pw", [P, D], ctx=ctx)
                pb = sb("pb", [P, D], ctx=ctx)
                g0 = sb("g0", [P, NT, D], ctx=ctx)
                gwT = sb("gwT", [P, E], ctx=ctx)
                dw = sb("dw", [P, HT, D], ctx=ctx)
                uw = sb("uw", [P, E, BN], ctx=ctx)
                db = sb("db", [P, HT], ctx=ctx)
                ub = sb("ub", [E, D], ctx=ctx)
                aoT = sb("aoT", [P, N], ctx=ctx)
                dwT = sb("dwT", [P, HT, P], ctx=ctx)
                uwT = sb("uwT", [P, HT, D], ctx=ctx)
                hg = sb("hg", [P, HT, N], ctx=ctx)
                xn = sb("xn1", [P, NT, D], ctx=ctx)
                stats = sb("stats1", [P, NT, 6], ctx=ctx)
                mv = sb("mv1", [P, NT, 2], ctx=ctx)
                std = sb("std1", [P, NT], ctx=ctx)
                rstd = sb("rstd1", [P, NT], ctx=ctx)
                pooled = sb("pooled", [P, 1], ctx=ctx)
                rt = sb("rt", [1, 16, E], ctx=ctx)
                wcol = sb("wcol", [P, HT], ctx=ctx)
                wrow = sb("wrow", [E, P], ctx=ctx)
                idx = sb("idx", [1, E], I32, ctx=ctx)
                pa = ps("pa1", [P, 2, 512], ctx)
                pp = ps("pp1", [P, 2, 512], ctx)
                pf = ps("pf1", [P, 2, 512], ctx)
                pr = ps("pr1", [P, 512], ctx)
                (in_p, turned, copied, proj_ready, dsteps, std_in, std_out, xn_ready, pooled_ready, logits_ready,
                 route_exp, route_in, route_ready, bcast_ready, wcol_ready, hid_ready, hid_done, f_ready, f_done,
                 idx_ready, zeros_set) = fresh(
                    ctx, "in_p", "turned1", "copied1", "proj_ready", "dsteps", "std_in", "std_out", "xn1_ready",
                    "pooled_ready", "logits_ready", "route_exp", "route_in", "route_ready", "bcast_ready", "wcol_ready",
                    "hid1_ready", "hid1_done", "f_ready", "f_done", "idx_ready", "zeros_set")
                with nc.Block() as block:
                    @block.sync
                    def _(sp):
                        with nc.allow_non_contiguous_dma("small weights"):
                            for dst, src in (
                                    (pw[:], A["L0_attn_proj_w"]), (pb[:], A["L0_attn_proj_b"].partition_broadcast(P)),
                                    (g0[:], g0_dram[:, bass.ds(batch * NT, NT), :]),
                                    (xb[:], A["L0_attn_x"].rearrange("b (t p) d -> p (b t) d", p=P)
                                     [:, bass.ds(batch * NT, NT), :]),
                                    (gwT[:], A["L1_ffn_gate_w"].rearrange("e d -> d e")),
                                    (dw[:], A["L1_ffn_down_w"].rearrange("e c d -> (e c) d")
                                     .rearrange("(m p) d -> p m d", p=P)),
                                    (uw[:], A["L1_ffn_up_w"].rearrange("e d c -> d e c")),
                                    (db[:], A["L1_ffn_down_b"].rearrange("e c -> (e c)")
                                     .rearrange("(m p) -> p m", p=P)),
                                    (ub[:], A["L1_ffn_up_b"])):
                                sp.dma_start(dst, src).then_inc(in_p, 16)
                    IN_P = 16 * 9

                    @block.gpsimd
                    def _(pool):
                        nc.gpsimd.memset(xnT[:, 0:MEM], 0.0).then_inc(zeros_set, 1)
                        nc.gpsimd.iota(idx[:], [[-1, E]], base=E, channel_multiplier=0).then_inc(idx_ready, 1)

                    @block.tensor
                    def _(pe):
                        for q in range(2):
                            for t in range(4 * q, 4 * q + 4):
                                mm = nc.tensor.transpose(pa[:, q, (t % 4) * P:(t % 4 + 1) * P], ao[:, t, :], ident[:])
                            mm.then_inc(turned, 1)
                        pe.wait_ge(in_p, IN_P)
                        for q in range(2):
                            pe.wait_ge(copied, q + 1)
                            for t in range(4 * q, 4 * q + 4):
                                mm = nc.tensor.matmul(pp[:, q, (t % 4) * P:(t % 4 + 1) * P], aoT[:, t * P:(t + 1) * P],
                                                      pw[:], start=True, stop=True)
                            mm.then_inc(proj_ready, 1)
                        for q, w in enumerate((dw[:], uw[:].rearrange("p e c -> p (e c)")
                                               .rearrange("p (m c) -> p m c", c=P))):
                            for m in range(HT):
                                mm = nc.tensor.transpose(pa[:, q, m * P:(m + 1) * P], w[:, m, :], ident[:])
                            mm.then_inc(turned, 1)
                        for q in range(2):
                            pe.wait_ge(copied, q + 3)
                            pe.wait_ge(xn_ready, q + 1)
                            for t in range(4 * q, 4 * q + 4):
                                mm = nc.tensor.transpose(pa[:, q, (t % 4) * P:(t % 4 + 1) * P], xn[:, t, :], ident[:])
                            mm.then_inc(turned, 1)
                        pe.wait_ge(pooled_ready, 1)
                        nc.tensor.matmul(pr[0:1, 0:E], pooled[:], gwT[:], start=True, stop=True).then_inc(logits_ready, 1)
                        for c in range(2):
                            for m in range(HT):
                                k = c * HT + m
                                if k >= 2:
                                    pe.wait_ge(hid_done, k - 1)
                                nc.tensor.matmul(pf[:, k % 2, :], dwT[:, m, :], xnT[:, MEM + c * 512:MEM + (c + 1) * 512],
                                                 start=True, stop=True).then_inc(hid_ready, 1)
                        pe.wait_ge(route_ready, 1)
                        nc.tensor.matmul(pr[:, 16:16 + E], ones1[0:1, :], rt[0:1, 15, :], start=True, stop=True)
                        nc.tensor.matmul(pr[0:E, 128:256], rt[0:1, 15, :], ones1[0:1, :], start=True, stop=True
                                         ).then_inc(bcast_ready, 1)
                        pe.wait_ge(wcol_ready, 1)
                        pe.wait_ge(hid_done, 2 * HT)
                        for q in range(2):
                            for t in range(4 * q, 4 * q + 4):
                                o = pf[:, q, (t % 4) * P:(t % 4 + 1) * P]
                                for m in range(HT):
                                    nc.tensor.matmul(o, hg[:, m, t * P:(t + 1) * P], uwT[:, m, :],
                                                     start=(m == 0), stop=False)
                                mm = nc.tensor.matmul(o, wrow[:], ub[:], start=False, stop=True)
                            mm.then_inc(f_ready, 1)

                    @block.scalar
                    def _(act):
                        for q in range(2):
                            act.wait_ge(turned, q + 1)
                            nc.scalar.copy(aoT[:, q * 512:(q + 1) * 512], pa[:, q, :]).then_inc(copied, 1)
                        for q, dst in enumerate((dwT, uwT)):
                            act.wait_ge(turned, q + 3)
                            nc.scalar.copy(dst[:], pa[:, q, :]).then_inc(copied, 1)
                        act.wait_ge(std_in, 1)
                        nc.scalar.activation(std[:], mv[:, :, 1], ACT.Sqrt).then_inc(std_out, 1)
                        for q in range(2):
                            act.wait_ge(turned, q + 5)
                            nc.scalar.copy(xnT[:, MEM + q * 512:MEM + (q + 1) * 512], pa[:, q, :]).then_inc(copied, 1)
                        act.wait_ge(route_in, 1)
                        nc.scalar.activation(rt[0:1, 2, :], rt[0:1, 0, :], ACT.Exp, bias=rt[0:1, 1, 0:1]
                                             ).then_inc(route_exp, 1)
                        for c in range(2):
                            for m in range(HT):
                                k = c * HT + m
                                act.wait_ge(hid_ready, k + 1)
                                nc.scalar.activation(hg[:, m, c * 512:(c + 1) * 512], pf[:, k % 2, :], ACT.Gelu,
                                                     bias=db[:, m:m + 1]).then_inc(hid_done, 1)
                        for q in range(2):
                            act.wait_ge(f_ready, q + 1)
                            nc.scalar.activation(g1[:, 4 * q:4 * q + 4, :], pf[:, q, :], ACT.Silu).then_inc(f_done, 1)

                    @block.vector
                    def _(dve):
                        n = [0]

                        def link(ins):
                            n[0] += 1
                            ins.then_inc(dsteps, 1)
                            dve.wait_ge(dsteps, n[0])

                        dve.wait_ge(in_p, IN_P)
                        for q in range(2):
                            dve.wait_ge(proj_ready, q + 1)
                            half = slice(4 * q, 4 * q + 4)
                            link(nc.vector.tensor_tensor(xn[:, half, :], pp[:, q, :].rearrange("p (t d) -> p t d", d=D),
                                                         pb[:].unsqueeze(1).to_broadcast([P, 4, D]), ALU.add))
                            link(nc.vector.tensor_tensor(xn[:, half, :], xn[:, half, :], g0[:, half, :], ALU.mult))
                            link(nc.vector.tensor_tensor(xb[:, half, :], xb[:, half, :], xn[:, half, :], ALU.add))
                        for t in range(NT):
                            ins = nc.vector.bn_stats(stats[:, t, :], xb[:, t, :])
                        link(ins)
                        for t in range(NT):
                            ins = nc.vector.bn_aggr(mv[:, t, :], stats[:, t, :])
                        link(ins)
                        nc.vector.tensor_scalar_add(mv[:, :, 1], mv[:, :, 1], 1e-5).then_inc(std_in, 1)
                        dve.wait_ge(std_out, 1)
                        link(nc.vector.reciprocal(rstd[:], std[:]))
                        for t in range(NT):
                            ins = nc.vector.tensor_scalar(xn[:, t, :], xb[:, t, :], mv[:, t, 0:1], rstd[:, t:t + 1],
                                                          ALU.subtract, ALU.mult)
                            if t % 4 == 3:
                                ins.then_inc(xn_ready, 1)
                        dve.wait_ge(copied, 6)
                        link(nc.vector.reduce_sum(pooled[:], xnT[:, MEM:KW], AX_X))
                        nc.vector.tensor_scalar(pooled[:], pooled[:], 1.0 / N, None, ALU.mult).then_inc(pooled_ready, 1)
                        dve.wait_ge(idx_ready, 1)
                        order = rt[0:1, 3, :]
                        link(nc.vector.tensor_copy(order, idx[:]))
                        dve.wait_ge(logits_ready, 1)
                        link(nc.vector.tensor_copy(rt[0:1, 0, :], pr[0:1, 0:E]))
                        link(nc.vector.reduce_max(rt[0:1, 1, 1:2], rt[0:1, 0, :], AX_X))
                        nc.vector.tensor_scalar(rt[0:1, 1, 0:1], rt[0:1, 1, 1:2], -1.0, None, ALU.mult
                                                ).then_inc(route_in, 1)
                        dve.wait_ge(route_exp, 1)
                        link(nc.vector.reduce_sum(rt[0:1, 1, 2:3], rt[0:1, 2, :], AX_X))
                        link(nc.vector.reciprocal(rt[0:1, 1, 3:4], rt[0:1, 1, 2:3]))
                        gate = rt[0:1, 4, :]
                        link(nc.vector.tensor_scalar(gate, rt[0:1, 2, :], rt[0:1, 1, 3:4], None, ALU.mult))
                        left, chosen = gate, []
                        for k in range(2):
                            top, pick, key, one, rest_of = (rt[0:1, 5 + 5 * k, k:k + 1], rt[0:1, 6 + 5 * k, 0:1],
                                                            rt[0:1, 7 + 5 * k, :], rt[0:1, 8 + 5 * k, :],
                                                            rt[0:1, 9, :])
                            link(nc.vector.reduce_max(top, left, AX_X))
                            link(nc.vector.tensor_scalar(key, left, top, None, ALU.is_equal))
                            link(nc.vector.tensor_tensor(key, key, order, ALU.mult))
                            link(nc.vector.reduce_max(pick, key, AX_X))
                            link(nc.vector.tensor_scalar(one, key, pick, None, ALU.is_equal))
                            chosen.append(one)
                            if k == 0:
                                link(nc.vector.tensor_scalar(rest_of, one, -2.0, None, ALU.mult))
                                link(nc.vector.tensor_tensor(rest_of, rest_of, gate, ALU.add))
                                left = rest_of
                        link(nc.vector.tensor_tensor(chosen[0], chosen[0], chosen[1], ALU.add))
                        link(nc.vector.tensor_tensor(gate, gate, chosen[0], ALU.mult))
                        link(nc.vector.reduce_sum(rt[0:1, 1, 4:5], gate, AX_X))
                        link(nc.vector.tensor_scalar(rt[0:1, 1, 4:5], rt[0:1, 1, 4:5], 1e-8, None, ALU.add))
                        link(nc.vector.reciprocal(rt[0:1, 1, 5:6], rt[0:1, 1, 4:5]))
                        nc.vector.tensor_scalar(rt[0:1, 15, :], gate, rt[0:1, 1, 5:6], None, ALU.mult
                                                ).then_inc(route_ready, 1)
                        dve.wait_ge(bcast_ready, 1)
                        for e in range(2):
                            link(nc.vector.tensor_copy(wcol[e * BN:(e + 1) * BN, :],
                                                       pr[e * BN:(e + 1) * BN, 16 + e:16 + E:2]))
                        link(nc.vector.tensor_copy(wrow[:], pr[0:E, 128:256]))
                        link(nc.vector.tensor_tensor(uwT[:], uwT[:], wcol[:].unsqueeze(2).to_broadcast([P, HT, D]),
                                                     ALU.mult))
                        dve.sem_inc(wcol_ready, 1)

            with ExitStack() as ctx:
                w3 = [sb(f"w3_{m}", [P, HW], ctx=ctx) for m in "qkv"]
                sq = sb("sq", [P, 2, 512], ctx=ctx)
                nr = sb("nr", [P, 2, 512], ctx=ctx)
                mk = sb("mk", [P, PAIRS, MEM], ctx=ctx)
                pq = ps("pq", [P, 2, 512], ctx)
                pn = ps("pn", [P, 2, 512], ctx)
                pv = ps("pv", [P, 4, 512], ctx)
                (in_w, q_ready, sq_ready, n_ready, nr_ready, q_done, msq, steps, v_ready, v_done, mem_in) = fresh(
                    ctx, "in_w", "q_ready", "sq_ready", "n_ready", "nr_ready", "q_done", "msq", "qkv_steps", "v_ready",
                    "v_done", "mem_in")
                UNITS = [(w, pr_, c) for w in range(2) for pr_ in range(PAIRS) for c in range(N // 512)]
                U = len(UNITS)
                QK_SCALE = 10.0

                with nc.Block() as block:
                    @block.sync
                    def _(sp):
                        for m, name in enumerate(("L1_attn_Wq", "L1_attn_Wk", "L1_attn_Wv")):
                            sp.dma_start(w3[m][:], A[name]).then_inc(in_w, 16)
                        with nc.allow_non_contiguous_dma("memory keys to channels on partitions"):
                            mkr = A["L1_attn_mem_k"].rearrange("(r two) m d -> two d r m", two=2)
                            for two in range(2):
                                for r in range(PAIRS):
                                    sp.dma_start(mk[two * DH1:(two + 1) * DH1, r, :], mkr[two, :, r, :]).then_inc(in_w, 16)
                        sp.wait_ge(v_done, 2)
                        sp.dma_start(vn[0:MEM, 0, :].rearrange("m (h d) -> m h d", d=DH1),
                                     A["L1_attn_mem_v"].rearrange("h m d -> m h d")).then_inc(mem_in, 16)
                        sp.wait_ge(mem_in, 16)
                    IN_W = 16 * (3 + 2 * PAIRS)

                    @block.tensor
                    def _(pe):
                        pe.wait_ge(in_w, IN_W)

                        def norm(u):
                            pe.wait_ge(sq_ready, u + 1)
                            if u >= 2:
                                pe.wait_ge(nr_ready, u - 1)
                            nc.tensor.matmul(pn[:, u % 2, :], headones[:], sq[:, u % 2, :], start=True, stop=True
                                             ).then_inc(n_ready, 1)

                        for u, (w, r, c) in enumerate(UNITS):
                            if u >= 2:
                                pe.wait_ge(q_done, u - 1)
                            nc.tensor.matmul(pq[:, u % 2, :], w3[w][:, r * P:(r + 1) * P],
                                             xnT[:, MEM + c * 512:MEM + (c + 1) * 512], start=True, stop=True
                                             ).then_inc(q_ready, 1)
                            if u >= 1:
                                norm(u - 1)
                        norm(U - 1)
                        pe.wait_ge(msq, 1)
                        pe.wait_ge(nr_ready, U)
                        nc.tensor.matmul(pn[:, 0, 0:PAIRS * MEM], headones[:], sq[:, 0, 0:PAIRS * MEM],
                                         start=True, stop=True).then_inc(n_ready, 1)
                        for k in range(2 * VB):
                            b, c = k // 2, k % 2
                            if k >= 4:
                                pe.wait_ge(v_done, k - 3)
                            nc.tensor.matmul(pv[0:rows_of[b], k % 4, :], xnT[:, first_of[b]:first_of[b] + rows_of[b]],
                                             w3[2][:, c * 512:(c + 1) * 512], start=True, stop=True).then_inc(v_ready, 1)

                    @block.scalar
                    def _(act):
                        def root(u, width):
                            act.wait_ge(n_ready, u + 1)
                            if 2 <= u < U:
                                act.wait_ge(q_done, u - 1)
                            nc.scalar.activation(nr[:, u % 2, 0:width], pn[:, u % 2, 0:width], ACT.Sqrt).then_inc(nr_ready, 1)

                        for u in range(U):
                            act.wait_ge(q_ready, u + 1)
                            if u >= 2:
                                act.wait_ge(n_ready, u - 1)
                            nc.scalar.activation(sq[:, u % 2, :], pq[:, u % 2, :], ACT.Square).then_inc(sq_ready, 1)
                            if u >= 1:
                                root(u - 1, 512)
                        root(U - 1, 512)
                        act.wait_ge(in_w, IN_W)
                        nc.scalar.activation(sq[:, 0, 0:PAIRS * MEM], mk[:], ACT.Square).then_inc(msq, 1)
                        act.wait_ge(q_done, U)
                        root(U, PAIRS * MEM)
                        for k in range(2 * VB):
                            b, c = k // 2, k % 2
                            act.wait_ge(v_ready, k + 1)
                            nc.scalar.copy(vn[0:rows_of[b], b, c * 512:(c + 1) * 512], pv[0:rows_of[b], k % 4, :]
                                           ).then_inc(v_done, 1)

                    @block.vector
                    def _(dve):
                        n = [0]

                        def link(ins):
                            n[0] += 1
                            ins.then_inc(steps, 1)
                            dve.wait_ge(steps, n[0])

                        for u, (w, r, c) in enumerate(UNITS):
                            root = nr[:, u % 2, :]
                            dve.wait_ge(nr_ready, u + 1)
                            link(nc.vector.tensor_scalar(root, root, 1e-12, None, ALU.max))
                            link(nc.vector.reciprocal(root, root))
                            dst = (qT[:, r, c * 512:(c + 1) * 512], kT[:, r, MEM + c * 512:MEM + (c + 1) * 512])[w]
                            nc.vector.scalar_tensor_tensor(dst, root, (QK_SCALE, 1.0)[w], pq[:, u % 2, :],
                                                           ALU.mult, ALU.mult).then_inc(q_done, 1)
                        dve.wait_ge(nr_ready, U + 1)
                        root = nr[:, 0, 0:PAIRS * MEM]
                        link(nc.vector.tensor_scalar(root, root, 1e-12, None, ALU.max))
                        link(nc.vector.reciprocal(root, root))
                        nc.vector.tensor_tensor(kT[:, :, 0:MEM], root.rearrange("p (r m) -> p r m", m=MEM), mk[:], ALU.mult)
            G = N // DH1
            UT = DH1 // IL
            PQ = UT // 2
            width = [MEM + DH1 * (s + 1) for s in range(G)]

            def pieces(s):
                k = -(-width[s] // 512)
                cut = [width[s] * i // k for i in range(k + 1)]
                return list(zip(cut[:-1], cut[1:]))

            def key_blocks(s):
                return [(k, rows_of[k] if k == 0 else min(P, width[s] - first_of[k]))
                        for k in range(VB) if first_of[k] < width[s]]

            def copies_of(s):
                whole = [k for k, rows in key_blocks(s) if rows == P]
                part = [[k] for k, rows in key_blocks(s) if rows != P]
                return part[:1] + [whole[i:i + 4] for i in range(0, len(whole), 4)] + part[1:]

            def before(f, s):
                return sum(UT * f(g) for g in range(s))

            n_pieces = [len(pieces(s)) for s in range(G)]
            n_copies = [len(copies_of(s)) for s in range(G)]

            with ExitStack() as ctx:
                aT = sb("aT", [P, VB, UT, P], ctx=ctx)
                qs = sb("qs", [P, 2, 4, 2, 32], ctx=ctx)
                dots = sb("dots", [P, 2, 512], ctx=ctx)
                xs = sb("xs", [P, 2, 2, KW], ctx=ctx)
                wk = sb("wk", [P, 2, KW], ctx=ctx)
                ex = sb("ex", [P, 2, KW], ctx=ctx)
                top64 = sb("top64", [P, 2, 8, 8], ctx=ctx)
                sc = sb("sc", [P, 2, 4], ctx=ctx)
                mix = sb("mix", [P, 2, P], ctx=ctx)
                pa = ps("pa2", [P, 2, 512], ctx)
                pb = ps("pb2", [P, 2, 512], ctx)
                pc = ps("pc2", [P, 2, 512], ctx)
                po = ps("po2", [P, PAIRS, DH1], ctx)
                (qs_zero, qs_ready, qk_ready, dots_ready, mixed, xs_ready, negmax, ex_ready, step, p_ready, turned,
                 at_ready, av_ready, av_done, gate, gate_act) = fresh(
                    ctx, "qs_zero", "qs_ready", "qk_ready", "dots_ready", "mixed", "xs_ready", "negmax", "ex_ready",
                    "dve_chain", "p_ready", "turned2", "at_ready", "av_ready", "av_done", "gate2", "gate_act")

                def at_least(eng, s, value):
                    if not isinstance(value, int) or value > 0:
                        eng.wait_ge(s, value)

                with nc.Block() as block:
                    @block.gpsimd
                    def _(pool):
                        nc.gpsimd.memset(qs[:], 0.0).then_inc(qs_zero, 1)
                        pool.wait_ge(qs_zero, 1)

                        def stage(s, i, j):
                            k = n_pieces[s]
                            if s == 0:
                                at_least(pool, dots_ready, (2 * i + j - 1) * k)
                            else:
                                at = before(lambda g: n_pieces[g], s)
                                back = k if j == 1 else 0
                                if isinstance(i, int) and i == 0 and j == 0:
                                    pool.wait_ge(dots_ready, at - n_pieces[s - 1])
                                else:
                                    pool.wait_ge(dots_ready, at + (2 * i + j - 1) * k)
                                    pool.sem_inc(gate, 1)
                            for p2 in range(2):
                                for half in range(2):
                                    part = slice(half * DH1, (half + 1) * DH1)
                                    c = (2 * p2 + half) * IL
                                    ins = nc.gpsimd.tensor_copy(
                                        qs[part, j, :, p2, c:c + IL],
                                        qT[part, p2:PAIRS:2, bass.ds(s * DH1 + (2 * i + j) * IL, IL)])
                            ins.then_inc(qs_ready, 1)

                        for s in range(G):
                            if s == 0:
                                for i in range(PQ):
                                    for j in range(2):
                                        stage(s, i, j)
                            else:
                                for j in range(2):
                                    stage(s, 0, j)
                                with pool.Fori(1, PQ) as i:
                                    for j in range(2):
                                        stage(s, i, j)

                    @block.tensor
                    def _(pe):
                        def front(s, i, j):
                            k, t = n_pieces[s], 2 * i + j
                            at = before(lambda g: n_pieces[g], s) + t * k
                            pe.wait_ge(qs_ready, s * UT + t + 1)
                            cols = pieces(s)
                            for n in range(k + 1):
                                if n < k:
                                    c0, c1 = cols[n]
                                    b = (j * k + n) % 2
                                    at_least(pe, dots_ready, at + n - 1)
                                    for p2 in range(2):
                                        for cg in range(4):
                                            mm = nc.tensor.matmul(pa[32 * cg:32 * cg + 32, b, 0:c1 - c0],
                                                                  qs[:, j, cg, p2, :], kT[:, 2 * cg + p2, c0:c1],
                                                                  start=(p2 == 0), stop=(p2 == 1))
                                    mm.then_inc(qk_ready, 1)
                                if n >= 1:
                                    c0, c1 = cols[n - 1]
                                    b = (j * k + n - 1) % 2
                                    pe.wait_ge(dots_ready, at + n)
                                    at_least(pe, xs_ready, at + n - 2)
                                    nc.tensor.matmul(pb[:, b, 0:c1 - c0], kron_pre[:].rearrange("p h i -> p (h i)"),
                                                     dots[:, b, 0:c1 - c0], start=True, stop=True).then_inc(mixed, 1)

                        def back(s, i, j):
                            t, k = 2 * i + j, n_copies[s]
                            at = before(lambda g: n_copies[g], s) + t * k
                            pe.wait_ge(p_ready, s * UT + t + 1)
                            for n, ks in enumerate(copies_of(s)):
                                b = (j * k + n) % 2
                                at_least(pe, at_ready, at + n - 1)
                                for m, kb in enumerate(ks):
                                    rows = dict(key_blocks(s))[kb]
                                    mm = nc.tensor.matmul(pc[0:rows, b, m * P:(m + 1) * P],
                                                          ex[:, j, first_of[kb]:first_of[kb] + rows], mix[:, j, :],
                                                          start=True, stop=True)
                                mm.then_inc(turned, 1)

                        def weigh(s):
                            pe.wait_ge(at_ready, before(lambda g: n_copies[g], s + 1))
                            at_least(pe, av_done, s)
                            blocks = key_blocks(s)
                            for r in range(PAIRS):
                                for k, rows in blocks:
                                    for half in range(2):
                                        h = 2 * r + half
                                        mm = nc.tensor.matmul(
                                            po[half * DH1:(half + 1) * DH1, r, :], vn[0:rows, k, h * DH1:(h + 1) * DH1],
                                            aT[0:rows, k, :, h * IL:(h + 1) * IL],
                                            start=(k == 0), stop=(k == blocks[-1][0]))
                            mm.then_inc(av_ready, 1)

                        for j in range(2):
                            front(0, 0, j)
                        for s in range(G):
                            def steady(i):
                                for j in range(2):
                                    front(s, i + 1, j)
                                for j in range(2):
                                    back(s, i, j)

                            if s == 0:
                                for i in range(PQ - 1):
                                    steady(i)
                            else:
                                with pe.Fori(0, PQ - 1) as i:
                                    steady(i)
                            if s + 1 < G:
                                for j in range(2):
                                    front(s + 1, 0, j)
                            for j in range(2):
                                back(s, PQ - 1, j)
                            weigh(s)

                    @block.scalar
                    def _(act):
                        def front(s, i, j):
                            k, t = n_pieces[s], 2 * i + j
                            at = before(lambda g: n_pieces[g], s) + t * k
                            const = isinstance(i, int)
                            for n, (c0, c1) in enumerate(pieces(s)):
                                b = (j * k + n) % 2
                                act.wait_ge(qk_ready, at + n + 1)
                                at_least(act, mixed, at + n - 1)
                                nc.scalar.copy(dots[:, b, 0:c1 - c0], pa[:, b, 0:c1 - c0]).then_inc(dots_ready, 1)
                                if n == 0:
                                    at_least(act, p_ready, (s * PQ + i - 1) * 2)
                                act.wait_ge(mixed, at + n + 1)
                                if not const:
                                    act.sem_inc(gate_act, 1)
                                q = (i % 2) if const else (i % 2)
                                dst = xs[:, q, j, c0:c1] if const else xs[:, bass.ds(q, 1), j, c0:c1]
                                nc.scalar.copy(dst, pb[:, b, 0:c1 - c0]).then_inc(xs_ready, 1)

                        def exps(s, i):
                            for j in range(2):
                                t = s * UT + 2 * i + j
                                const = isinstance(i, int)
                                act.wait_ge(negmax, t + 1)
                                if const and i == 0:
                                    if s > 0:
                                        act.wait_ge(turned, before(lambda g: n_copies[g], s) - n_copies[s - 1] * (1 - j))
                                else:
                                    act.wait_ge(turned, before(lambda g: n_copies[g], s)
                                                + (2 * i + j - 1) * n_copies[s])
                                if not const:
                                    act.sem_inc(gate_act, 1)
                                q = i % 2
                                src = xs[:, q, j, 0:width[s]] if const else xs[:, bass.ds(q, 1), j, 0:width[s]]
                                nc.scalar.activation(ex[:, j, 0:width[s]], src, ACT.Exp,
                                                     bias=sc[:, j, 0:1]).then_inc(ex_ready, 1)

                        def back(s, i, j):
                            t, k = 2 * i + j, n_copies[s]
                            at = before(lambda g: n_copies[g], s) + t * k
                            const = isinstance(i, int)
                            for n, ks in enumerate(copies_of(s)):
                                b = (j * k + n) % 2
                                rows = dict(key_blocks(s))[ks[0]]
                                act.wait_ge(turned, at + n + 1)
                                if not const:
                                    act.sem_inc(gate_act, 1)
                                at_u = t if const else bass.ds(t, 1)
                                src = pc[0:rows, b, 0:len(ks) * P]
                                dst = (aT[0:rows, ks[0]:ks[-1] + 1, at_u, :])
                                nc.scalar.copy(dst, src.rearrange("p (k c) -> p k c", c=P)).then_inc(at_ready, 1)

                        def steady(s, i):
                            exps(s, i)
                            for j in range(2):
                                front(s, i + 1, j)
                            for j in range(2):
                                back(s, i, j)

                        for j in range(2):
                            front(0, 0, j)
                        for s in range(G):
                            if s == 0:
                                for i in range(PQ - 1):
                                    steady(s, i)
                            else:
                                steady(s, 0)
                                with act.Fori(1, PQ - 1) as i:
                                    steady(s, i)
                            exps(s, PQ - 1)
                            if s + 1 < G:
                                for j in range(2):
                                    front(s + 1, 0, j)
                            for j in range(2):
                                back(s, PQ - 1, j)
                            act.wait_ge(av_ready, s + 1)
                            nc.scalar.copy(qT[:, :, s * DH1:(s + 1) * DH1], po[:]).then_inc(av_done, 1)

                    @block.vector
                    def _(dve):
                        CHAIN = 2 * (1 + 8 + 7 + 2)

                        def pair(s, i, parity):
                            n = [parity * CHAIN]
                            w = width[s]

                            def do(ins):
                                n[0] += 1
                                return ins.then_inc(step, 1)

                            x = [xs[:, parity, j, 0:w] for j in range(2)]
                            u = [wk[:, j, 0:w] for j in range(2)]
                            for j in range(2):
                                t = 2 * i + j
                                dve.wait_ge(xs_ready, before(lambda g: n_pieces[g], s) + (t + 1) * n_pieces[s])
                                at = (UT - 1) * IL - t * IL
                                m = slide[:, bass.ds(at, DH1)] if not isinstance(at, int) else slide[:, at:at + DH1]
                                do(nc.vector.tensor_tensor(xs[:, parity, j, w - DH1:w], xs[:, parity, j, w - DH1:w],
                                                           m, ALU.add))
                            for r in range(8):
                                for j in range(2):
                                    dve.wait_ge(step, n[0] - 1)
                                    do(nc.vector.max(top64[:, j, r, :], x[j] if r == 0 else u[j]))
                                if r == 0:
                                    for j in range(2):
                                        dve.wait_ge(step, n[0] - 1 + j)
                                        nc.vector.tensor_scalar(sc[:, j, 0:1], top64[:, j, 0, 0:1], -1.0, None,
                                                                ALU.mult).then_inc(negmax, 1)
                                if r == 7:
                                    break
                                for j in range(2):
                                    dve.wait_ge(step, n[0] - 1)
                                    do(nc.vector.match_replace(u[j], top64[:, j, r, :], x[j] if r == 0 else u[j], -BIG))
                            for j in range(2):
                                dve.wait_ge(ex_ready, s * UT + 2 * i + j + 1)
                                dve.wait_ge(step, n[0] - 1)
                                nc.vector.scalar_tensor_tensor(ex[:, j, 0:w], x[j], top64[:, j, 7, 7:8], ex[:, j, 0:w],
                                                               ALU.is_ge, ALU.mult, accum_out=sc[:, j, 1:2]
                                                               ).then_inc(step, 1)
                                n[0] += 1
                            for j in range(2):
                                dve.wait_ge(step, n[0] - 1)
                                do(nc.vector.reciprocal(sc[:, j, 2:3], sc[:, j, 1:2]))
                            for j in range(2):
                                dve.wait_ge(step, n[0] - 1 + j)
                                nc.vector.tensor_scalar(mix[:, j, :], kron_post[:].rearrange("p h i -> p (h i)"),
                                                        sc[:, j, 2:3], None, ALU.mult).then_inc(p_ready, 1)
                            return n[0]

                        for s in range(G):
                            with dve.Fori(0, PQ // 2) as i2:
                                dve.sem_clear(step)
                                pair(s, 2 * i2, 0)
                                total = pair(s, 2 * i2 + 1, 1)
                                dve.wait_ge(step, total)

            with ExitStack() as ctx:
                wg = sb("wg", [P, HW], ctx=ctx)
                wo = sb("wo", [P, PAIRS, D], ctx=ctx)
                bgc = sb("bgc", [P, PAIRS], ctx=ctx)
                hs = sb("hs", [P, PAIRS], ctx=ctx)
                sig = sb("sig", [P, 2, N], ctx=ctx)
                res = sb("res", [P, NT, D], ctx=ctx)
                pz = ps("pz", [P, 2, N], ctx)
                py = ps("py", [P, 2, 512], ctx)
                (in_g, z_ready, sig_ready, gated, y_ready, s_done, res_ready, out_stored) = fresh(
                    ctx, "in_g", "z_ready", "sig_ready", "gated", "y_ready", "s_done", "res_ready", "out_stored")
                with nc.Block() as block:
                    @block.sync
                    def _(sp):
                        with nc.allow_non_contiguous_dma("a bias and a scale for each channel"):
                            sp.dma_start(wg[:], A["L1_attn_Wg"]).then_inc(in_g, 16)
                            sp.dma_start(wo[:], A["L1_attn_Wo"].rearrange("(r p) d -> p r d", p=P)).then_inc(in_g, 16)
                            sp.dma_start(bgc[:], A["L1_attn_bg"].rearrange("(r p) -> p r", p=P)).then_inc(in_g, 16)
                            scale = A["L1_attn_head_scale_params"].rearrange("a (r two) b c -> two (a r b c)", two=2)
                            for two in range(2):
                                sp.dma_start(hs[two * DH1:(two + 1) * DH1, :], scale[two].partition_broadcast(DH1)
                                             ).then_inc(in_g, 16)
                        for q in range(2):
                            sp.wait_ge(res_ready, q + 1)
                            sp.dma_start(out.rearrange("b (t p) d -> p (b t) d", p=P)
                                         [:, bass.ds(batch * NT + 4 * q, 4), :], res[:, 4 * q:4 * q + 4, :]
                                         ).then_inc(out_stored, 16)
                        sp.wait_ge(out_stored, 32)

                    @block.tensor
                    def _(pe):
                        pe.wait_ge(in_g, 16 * 5)
                        for r in range(PAIRS):
                            if r >= 2:
                                pe.wait_ge(sig_ready, r - 1)
                            for c in range(2):
                                mm = nc.tensor.matmul(pz[:, r % 2, c * 512:(c + 1) * 512], wg[:, r * P:(r + 1) * P],
                                                      xnT[:, MEM + c * 512:MEM + (c + 1) * 512], start=True, stop=True)
                            mm.then_inc(z_ready, 1)
                        pe.wait_ge(gated, PAIRS)
                        for q in range(2):
                            for t in range(4 * q, 4 * q + 4):
                                for r in range(PAIRS):
                                    mm = nc.tensor.matmul(py[:, q, (t % 4) * P:(t % 4 + 1) * P], qT[:, r, t * P:(t + 1) * P],
                                                          wo[:, r, :], start=(r == 0), stop=(r == PAIRS - 1))
                            mm.then_inc(y_ready, 1)

                    @block.scalar
                    def _(act):
                        for r in range(PAIRS):
                            act.wait_ge(z_ready, r + 1)
                            if r >= 2:
                                act.wait_ge(gated, r - 1)
                            nc.scalar.activation(sig[:, r % 2, :], pz[:, r % 2, :], ACT.Sigmoid, bias=bgc[:, r:r + 1]
                                                 ).then_inc(sig_ready, 1)

                    @block.vector
                    def _(dve):
                        for r in range(PAIRS):
                            dve.wait_ge(sig_ready, r + 1)
                            nc.vector.scalar_tensor_tensor(qT[:, r, :], sig[:, r % 2, :], hs[:, r:r + 1], qT[:, r, :],
                                                           ALU.mult, ALU.mult).then_inc(gated, 1)
                        for q in range(2):
                            half = slice(4 * q, 4 * q + 4)
                            dve.wait_ge(y_ready, q + 1)
                            nc.vector.tensor_tensor(res[:, half, :], py[:, q, :].rearrange("p (t d) -> p t d", d=D),
                                                    g1[:, half, :], ALU.mult).then_inc(s_done, 1)
                            dve.wait_ge(s_done, q + 1)
                            nc.vector.tensor_tensor(res[:, half, :], res[:, half, :], xb[:, half, :],
                                                    ALU.add).then_inc(res_ready, 1)


def kernel(**inputs):
    import numpy as np
    import concourse.bacc as bacc
    from concourse.bass_utils import run_bass_kernel_spmd

    nc = bacc.Bacc("TRN2", target_bir_lowering=False, num_devices=1)
    arrays = {f"in_{name}": np.ascontiguousarray(a) for name, a in inputs.items()}
    A = {name: nc.dram_tensor(f"in_{name}", a.shape, mybir.dt.from_np(a.dtype), kind="ExternalInput").ap()
         for name, a in ((n, arrays[f"in_{n}"]) for n in inputs)}
    out = nc.dram_tensor("out_dram", inputs["L0_attn_x"].shape, F32, kind="ExternalOutput").ap()
    program(nc, A, out)
    got = run_bass_kernel_spmd(nc, [arrays], core_ids=[0])
    return got.results[0]["out_dram"]
```

```python
from contextlib import ExitStack

import concourse.bass as bass
from concourse import mybir

ALU = mybir.AluOpType
ACT = mybir.ActivationFunctionType
F32 = mybir.dt.float32
BF16 = mybir.dt.bfloat16
I32 = mybir.dt.int32
AX_X = mybir.AxisListType.X
RMAX = bass.bass_isa.ReduceOp.max
RADD = bass.bass_isa.ReduceOp.add

P = 128
BIG = 3.4028234663852886e38
ROUND = 12582912.0
QB = 128.0


def program(nc, A, out, debug=None):
    B, N, D = A["L0_attn_x"].shape
    HID = A["L0_attn_q_w1"].shape[1]
    HT = HID // P
    H = A["L1_attn_W_pre_th"].shape[0]
    DH0 = D // H
    HW = A["L1_attn_Wq"].shape[1]
    DH1 = HW // H
    MEM = A["L1_attn_mem_k"].shape[1]
    E, BN, _ = A["L1_ffn_down_w"].shape
    NT = N // P
    T = B * NT
    PAIRS = H // 2
    IL = P // H
    SPLITS = 3
    KR = SPLITS * SPLITS * DH0
    KW = MEM + N
    TOPK = 64
    ROUNDS = 4
    PICK = 8 * ROUNDS

    with ExitStack() as top:
        def sb(name, shape, dt=F32, ctx=top):
            return ctx.enter_context(nc.sbuf_tensor(name, shape, dt))

        def ps(name, shape, ctx, dt=F32):
            return ctx.enter_context(nc.psum_tensor(name, shape, dt))

        def sem(name, ctx=top):
            return ctx.enter_context(nc.semaphore(name))

        ident = sb("ident", [P, P])
        d8 = sb("d8", [P, IL])
        d32 = sb("d32", [P, 32])
        headones = sb("headones", [P, P])
        ones1 = sb("ones1", [P, P])
        slide = sb("slide", [P, 2 * DH1 - IL])
        kron_pre = sb("kron_pre", [P, H, IL])
        kron_post = sb("kron_post", [P, H, IL])
        ranks = sb("ranks", [P, PICK])

        xnT_dram = nc.dram_tensor("xnT_dram", [P, T * P], F32, kind="Internal").ap()
        g0_dram = nc.dram_tensor("g0_dram", [P, T, D], F32, kind="Internal").ap()

        with ExitStack() as ctx:
            x_all = sb("x_all", [P, T, D], ctx=ctx)
            xnT_all = sb("xnT_all", [P, T * P], ctx=ctx)
            g0_all = sb("g0_all", [P, T, D], ctx=ctx)
            wq8 = sb("wq8", [P, D], ctx=ctx)
            fw = sb("fw", [P, D], ctx=ctx)
            lng = sb("lng", [P, D], ctx=ctx)
            lnb = sb("lnb", [P, D], ctx=ctx)
            wpre = sb("wpre", [P, H], ctx=ctx)
            wpost = sb("wpost", [P, H], ctx=ctx)
            stats = sb("stats", [P, T, 6], ctx=ctx)
            mv = sb("mv", [P, T, 2], ctx=ctx)
            stats2 = sb("stats2", [P, T, 6], ctx=ctx)
            mv2 = sb("mv2", [P, T, 2], ctx=ctx)
            std = sb("std", [P, 2, T], ctx=ctx)
            rstd = sb("rstd", [P, 2, T], ctx=ctx)
            xn = sb("xn", [P, T, D], ctx=ctx)
            xq = sb("xq", [P, T, D], ctx=ctx)
            scratch = sb("scratch", [P, T, D], ctx=ctx)
            xqT = sb("xqT", [P, T * P], ctx=ctx)
            amax = sb("amax", [P, 1], ctx=ctx)
            gmax = sb("gmax", [P, 1], ctx=ctx)
            asum = sb("asum", [P, 1], ctx=ctx)
            gsum = sb("gsum", [P, 1], ctx=ctx)
            cols = sb("cols", [P, 8], ctx=ctx)
            icol = sb("icol", [P, 2 * DH1 - IL], I32, ctx=ctx)
            fcol = sb("fcol", [P, 2 * DH1 - IL], ctx=ctx)
            irow = sb("irow", [P, IL], I32, ctx=ctx)
            frow = sb("frow", [P, IL], ctx=ctx)
            il = sb("il", [P, 1], ctx=ctx)
            ps_t = ps("ps_t", [P, 4, 512], ctx)
            ps_y = ps("ps_y", [P, 4, 512], ctx)

            x_in = sem("x_in", ctx)
            w_in = sem("w_in", ctx)
            consts = sem("consts", ctx)
            reduced = sem("reduced", ctx)
            dve_step = sem("dve_step", ctx)
            var_ready = sem("var_ready", ctx)
            std_ready = sem("std_ready", ctx)
            xn_ready = sem("xn_ready", ctx)
            xn2_ready = sem("xn2_ready", ctx)
            abs_ready = sem("abs_ready", ctx)
            wabs_ready = sem("wabs_ready", ctx)
            sums_ready = sem("sums_ready", ctx)
            xq_ready = sem("xq_ready", ctx)
            wq_ready = sem("wq_ready", ctx)
            turned = sem("turned", ctx)
            xnT_done = sem("xnT_done", ctx)
            xqT_done = sem("xqT_done", ctx)
            y_ready = sem("y_ready", ctx)
            gate_done = sem("gate_done", ctx)
            stored = sem("stored", ctx)

            block = ctx.enter_context(nc.Block())

            @block.sync
            def _(sp):
                xr = A["L0_attn_x"].rearrange("b (t p) d -> p (b t) d", p=P)
                sp.dma_start(x_all[:], xr).then_inc(x_in, 16)
                sp.dma_start(fw[:], A["L0_ffn_weight"]).then_inc(w_in, 16)
                sp.dma_start(lng[:], A["L0_ffn_ln_gamma"].partition_broadcast(P)).then_inc(w_in, 16)
                sp.dma_start(lnb[:], A["L0_ffn_ln_beta"].partition_broadcast(P)).then_inc(w_in, 16)
                with nc.allow_non_contiguous_dma("2048 single weights, once"):
                    for i in range(IL):
                        for w, t in (("L1_attn_W_pre_th", wpre), ("L1_attn_W_post_th", wpost)):
                            sp.dma_start(t[i:P:IL, :], A[w].rearrange("h g -> g h")).then_inc(w_in, 16)

                sp.wait_ge(xnT_done, T // 4)
                sp.dma_start(xnT_dram, xnT_all[:]).then_inc(stored, 16)
                sp.wait_ge(gate_done, T // 4)
                sp.dma_start(g0_dram, g0_all[:]).then_inc(stored, 16)
                sp.wait_ge(stored, 32)

            WEIGHTS_IN = 16 * (3 + 2 * IL)

            @block.gpsimd
            def _(pool):
                nc.gpsimd.memset(ident[:], 0.0).then_inc(consts, 1)
                pool.wait_ge(consts, 1)
                nc.gpsimd.affine_select(out=ident[:], in_=ident[:], compare_op=ALU.not_equal, fill=1.0, base=0,
                                        pattern=[[-1, P]], channel_multiplier=1).then_inc(consts, 1)
                nc.gpsimd.iota(icol[:], [[1, 2 * DH1 - IL]], base=IL - DH1, channel_multiplier=0).then_inc(consts, 1)
                nc.gpsimd.iota(irow[:], [[1, IL]], base=0, channel_multiplier=0).then_inc(consts, 1)
                nc.gpsimd.memset(ones1[:], 1.0).then_inc(consts, 1)
                pool.wait_ge(sums_ready, 1)
                nc.gpsimd.partition_all_reduce(gsum[:], asum[:], P, RADD).then_inc(reduced, 1)
                pool.wait_ge(sums_ready, 2)
                nc.gpsimd.partition_all_reduce(gmax[:], amax[:], P, RMAX).then_inc(reduced, 1)

            @block.scalar
            def _(act):
                act.wait_ge(w_in, WEIGHTS_IN)
                nc.scalar.activation(wq8[:], fw[:], ACT.Abs).then_inc(wabs_ready, 1)
                for k in range(2):
                    act.wait_ge(var_ready, k + 1)
                    nc.scalar.activation(std[:, k, :], (mv, mv2)[k][:, :, 1], ACT.Sqrt).then_inc(std_ready, 1)
                for q in range(T // 4):
                    act.wait_ge(turned, q + 1)
                    nc.scalar.copy(xnT_all[:, q * 512:(q + 1) * 512], ps_t[:, q, :]).then_inc(xnT_done, 1)
                act.wait_ge(xn2_ready, 1)
                nc.scalar.activation(scratch[:], xq[:], ACT.Abs).then_inc(abs_ready, 1)
                for q in range(T // 4):
                    act.wait_ge(turned, T // 4 + q + 1)
                    nc.scalar.copy(xqT[:, q * 512:(q + 1) * 512], ps_t[:, q, :]).then_inc(xqT_done, 1)
                act.wait_ge(wq_ready, 1)
                for q in range(T // 4):
                    act.wait_ge(y_ready, q + 1)
                    nc.scalar.activation(g0_all[:, 4 * q:4 * q + 4, :], ps_y[:, q, :], ACT.Silu,
                                         scale=cols[:, 4:5]).then_inc(gate_done, 1)

            @block.vector
            def _(dve):
                steps = [0]

                def link(ins):
                    steps[0] += 1
                    ins.then_inc(dve_step, 1)
                    dve.wait_ge(dve_step, steps[0])

                nc.vector.memset(headones[:], 0.0).then_inc(dve_step, 1)
                steps[0] = 1
                dve.wait_ge(dve_step, 1)
                nc.vector.memset(headones[0:DH1, 0:DH1], 1.0).then_inc(dve_step, 1)
                nc.vector.memset(headones[DH1:P, DH1:P], 1.0).then_inc(dve_step, 1)
                steps[0] = 3
                dve.wait_ge(x_in, 16)
                for t in range(T):
                    ins = nc.vector.bn_stats(stats[:, t, :], x_all[:, t, :])
                link(ins)
                for t in range(T):
                    ins = nc.vector.bn_aggr(mv[:, t, :], stats[:, t, :])
                link(ins)
                nc.vector.tensor_scalar_add(mv[:, :, 1], mv[:, :, 1], 1e-5).then_inc(var_ready, 1)
                dve.wait_ge(wabs_ready, 1)
                nc.vector.reduce_sum(asum[:], wq8[:], AX_X).then_inc(sums_ready, 1)
                dve.wait_ge(consts, 5)
                link(nc.vector.reduce_sum(d8[:], ident[:].rearrange("p (g i) -> p i g", i=IL), AX_X))
                link(nc.vector.reduce_sum(d32[:], ident[:].rearrange("p (g i) -> p i g", i=32), AX_X))
                link(nc.vector.tensor_copy(frow[:], irow[:]))
                link(nc.vector.tensor_copy(fcol[:], icol[:]))
                link(nc.vector.tensor_tensor(frow[:], frow[:], d8[:], ALU.mult))
                link(nc.vector.reduce_sum(il[:], frow[:], AX_X))
                link(nc.vector.tensor_scalar(slide[:], fcol[:], il[:, 0:1], -BIG, ALU.is_gt, ALU.mult))
                link(nc.vector.tensor_scalar(ranks[:], fcol[:, 0:PICK], -1.0, float(TOPK - 1 - (DH1 - IL)),
                                             ALU.mult, ALU.add))
                dve.wait_ge(w_in, WEIGHTS_IN)
                for src, kron in ((wpre, kron_pre), (wpost, kron_post)):
                    link(nc.vector.tensor_tensor(kron[:], src[:].unsqueeze(2).to_broadcast([P, H, IL]),
                                                 d8[:].unsqueeze(1).to_broadcast([P, H, IL]), ALU.mult))
                dve.wait_ge(std_ready, 1)
                link(nc.vector.reciprocal(rstd[:, 0, :], std[:, 0, :]))
                for t in range(T):
                    ins = nc.vector.tensor_scalar(xn[:, t, :], x_all[:, t, :], mv[:, t, 0:1], rstd[:, 0, t:t + 1],
                                                  ALU.subtract, ALU.mult)
                    if t % 4 == 3:
                        ins.then_inc(xn_ready, 1)
                dve.wait_ge(xn_ready, T // 4)
                for t in range(T):
                    ins = nc.vector.bn_stats(stats2[:, t, :], xn[:, t, :])
                link(ins)
                for t in range(T):
                    ins = nc.vector.bn_aggr(mv2[:, t, :], stats2[:, t, :])
                link(ins)
                nc.vector.tensor_scalar_add(mv2[:, :, 1], mv2[:, :, 1], 1e-3).then_inc(var_ready, 1)
                dve.wait_ge(std_ready, 2)
                link(nc.vector.reciprocal(rstd[:, 1, :], std[:, 1, :]))
                for t in range(T):
                    ins = nc.vector.tensor_scalar(xq[:, t, :], xn[:, t, :], mv2[:, t, 0:1], rstd[:, 1, t:t + 1],
                                                  ALU.subtract, ALU.mult)
                link(ins)
                link(nc.vector.tensor_tensor(xq[:], xq[:], lng[:].unsqueeze(1).to_broadcast([P, T, D]), ALU.mult))
                nc.vector.tensor_tensor(xq[:], xq[:], lnb[:].unsqueeze(1).to_broadcast([P, T, D]),
                                        ALU.add).then_inc(xn2_ready, 1)
                dve.wait_ge(abs_ready, 1)
                nc.vector.reduce_max(amax[:], scratch[:].rearrange("p t d -> p (t d)"), AX_X).then_inc(sums_ready, 1)
                dve.wait_ge(reduced, 1)
                link(nc.vector.tensor_scalar(cols[:, 0:1], gsum[:], 1.0 / (D * D), None, ALU.mult))
                link(nc.vector.tensor_scalar(cols[:, 1:2], cols[:, 0:1], 1e-5, None, ALU.add))
                link(nc.vector.reciprocal(cols[:, 2:3], cols[:, 1:2]))
                link(nc.vector.tensor_scalar(wq8[:], fw[:], cols[:, 2:3], ROUND, ALU.mult, ALU.add))
                link(nc.vector.tensor_scalar(wq8[:], wq8[:], ROUND, 1.0, ALU.subtract, ALU.min))
                link(nc.vector.tensor_scalar(wq8[:], wq8[:], -1.0, None, ALU.max))
                dve.wait_ge(reduced, 2)
                link(nc.vector.reciprocal(cols[:, 3:4], gmax[:]))
                link(nc.vector.tensor_scalar(cols[:, 3:4], cols[:, 3:4], QB, None, ALU.mult))
                link(nc.vector.tensor_scalar(xq[:], xq[:], cols[:, 3:4], QB - 1e-5, ALU.mult, ALU.min))
                nc.vector.tensor_scalar(xq[:], xq[:], -QB + 1e-5, None, ALU.max).then_inc(xq_ready, 1)
                link(nc.vector.tensor_tensor(cols[:, 4:5], gmax[:], cols[:, 0:1], ALU.mult))
                nc.vector.tensor_scalar(cols[:, 4:5], cols[:, 4:5], 1.0 / QB, None, ALU.mult).then_inc(wq_ready, 1)

            @block.tensor
            def _(pe):
                pe.wait_ge(consts, 2)
                for q in range(T // 4):
                    pe.wait_ge(xn_ready, q + 1)
                    for t in range(4 * q, 4 * q + 4):
                        mm = nc.tensor.transpose(ps_t[:, q, (t % 4) * P:(t % 4 + 1) * P], xn[:, t, :], ident[:])
                    mm.then_inc(turned, 1)
                pe.wait_ge(xq_ready, 1)
                for q in range(T // 4):
                    pe.wait_ge(xnT_done, q + 1)
                    for t in range(4 * q, 4 * q + 4):
                        mm = nc.tensor.transpose(ps_t[:, q, (t % 4) * P:(t % 4 + 1) * P], xq[:, t, :], ident[:])
                    mm.then_inc(turned, 1)
                pe.wait_ge(wq_ready, 1)
                for q in range(T // 4):
                    pe.wait_ge(xqT_done, q + 1)
                    for t in range(4 * q, 4 * q + 4):
                        mm = nc.tensor.matmul(ps_y[:, q, (t % 4) * P:(t % 4 + 1) * P], xqT[:, t * P:(t + 1) * P],
                                              wq8[:], start=True, stop=True)
                    mm.then_inc(y_ready, 1)

        qk_parts = nc.dram_tensor("qk_parts", [2, SPLITS, P, N], BF16, kind="Internal").ap()

        def fresh(ctx, *names):
            sems = [sem(n, ctx) for n in names]
            with nc.Block() as reset:
                @reset.gpsimd
                def _(pool):
                    for s in sems:
                        pool.sem_clear(s)
            return sems

        with nc.Fori(0, B) as batch, ExitStack() as per_batch:
            ao = sb("ao", [P, NT, D], ctx=per_batch)

            with ExitStack() as layer0:
                va = sb("va", [P, NT, H, DH0 + 1], ctx=layer0)
                qsp = sb("qsp", [KR + 2, H, N], BF16, ctx=layer0)
                ksp = sb("ksp", [KR + 2, H, N], BF16, ctx=layer0)

                with ExitStack() as ctx:
                    xnT0 = sb("xnT0", [P, N], ctx=ctx)
                    w1 = [sb(f"{m}_w1", [P, HID], ctx=ctx) for m in "qkv"]
                    w2 = [sb(f"{m}_w2", [P, HT, D], ctx=ctx) for m in "qkv"]
                    b1 = sb("b1", [P, 3, HT], ctx=ctx)
                    b2 = sb("b2", [P, 2], ctx=ctx)
                    b2v = sb("b2v", [P, D], ctx=ctx)
                    hid = sb("hid", [P, 2, HT, 512], ctx=ctx)
                    rest = sb("rest", [P, 3, 512], ctx=ctx)
                    parts = sb("parts", [P, 2, SPLITS, N], BF16, ctx=ctx)
                    ps_h = ps("ps_h", [P, HT, 512], ctx)
                    ps_o = ps("ps_o", [P, 2, 512], ctx)
                    (q_in, k_in, v_in, ones_set, hid_ready, gelu_done, out_ready, out_read, parts_stored, spread_in,
                     step) = fresh(ctx, "q_in", "k_in", "v_in", "ones_set", "hid_ready", "gelu_done", "out_ready", "out_read",
                                   "parts_stored", "spread_in", "mlp_step")
                    there = (q_in, k_in, v_in)
                    LOADS = (5, 4, 4)
                    STEPS = [(m, c) for m in range(3) for c in range(N // 512)]
                    SCALE = float(DH0) ** -0.5

                    with nc.Block() as block:
                        @block.sync
                        def _(sp):
                            sp.dma_start(xnT0[:], xnT_dram[:, bass.ds(batch * N, N)]).then_inc(q_in, 16)
                            with nc.allow_non_contiguous_dma("biases, one value a partition"):
                                for m, name in enumerate("qkv"):
                                    sp.dma_start(w1[m][:], A[f"L0_attn_{name}_w1"]).then_inc(there[m], 16)
                                    sp.dma_start(b1[:, m, :], A[f"L0_attn_{name}_b1"].rearrange("(i p) -> p i", p=P)
                                                 ).then_inc(there[m], 16)
                                    sp.dma_start(w2[m][:], A[f"L0_attn_{name}_w2"].rearrange("(i p) d -> p i d", p=P)
                                                 ).then_inc(there[m], 16)
                                    if m < 2:
                                        sp.dma_start(b2[:, m:m + 1], A[f"L0_attn_{name}_b2"]
                                                     .rearrange("(p o) -> p o", o=1)).then_inc(there[m], 16)
                                sp.dma_start(b2v[:], A["L0_attn_v_b2"].partition_broadcast(P)).then_inc(v_in, 16)
                            for m in range(2):
                                sp.wait_ge(out_read, 2 * (m + 1))
                                sp.dma_start(qk_parts[m].rearrange("j p n -> p j n"), parts[:, m]
                                             ).then_inc(parts_stored, 16)
                            sp.wait_ge(ones_set, 2)
                            for m, dst in enumerate((qsp, ksp)):
                                sp.wait_ge(parts_stored, 16 * 2)
                                for i in range(SPLITS):
                                    for j in range(SPLITS):
                                        r = (SPLITS * i + j) * DH0
                                        src = qk_parts[m, (i, j)[m]].rearrange("(h d) n -> d h n", d=DH0)
                                        sp.dma_start(dst[r:r + DH0], src).then_inc(spread_in, 16)
                            sp.wait_ge(spread_in, 16 * 2 * SPLITS * SPLITS)

                        @block.gpsimd
                        def _(pool):
                            nc.gpsimd.memset(va[:, :, :, DH0:DH0 + 1], 1.0).then_inc(ones_set, 1)
                            pool.wait_ge(ones_set, 1)
                            nc.gpsimd.memset(ksp[KR - DH0:KR + 2], 1.0).then_inc(ones_set, 1)

                        @block.tensor
                        def _(pe):
                            for s in range(len(STEPS) + 1):
                                if s < len(STEPS):
                                    m, c = STEPS[s]
                                    if c == 0:
                                        pe.wait_ge(there[m], 16 * LOADS[m])
                                    for i in range(HT):
                                        if s >= 1:
                                            pe.wait_ge(gelu_done, HT * (s - 1) + i + 1)
                                        nc.tensor.matmul(ps_h[:, i, :], w1[m][:, i * P:(i + 1) * P],
                                                         xnT0[:, c * 512:(c + 1) * 512],
                                                         start=True, stop=True).then_inc(hid_ready, 1)
                                if s >= 1:
                                    m, c = STEPS[s - 1]
                                    pe.wait_ge(gelu_done, HT * s)
                                    if s >= 3:
                                        pe.wait_ge(out_read, s - 2)
                                    o = ps_o[:, (s - 1) % 2, :]
                                    h = hid[:, (s - 1) % 2]
                                    if m < 2:
                                        for i in range(HT):
                                            mm = nc.tensor.matmul(o, w2[m][:, i, :], h[:, i, :],
                                                                  start=(i == 0), stop=(i == HT - 1))
                                    else:
                                        for t in range(4):
                                            for i in range(HT):
                                                mm = nc.tensor.matmul(o[:, t * P:(t + 1) * P], h[:, i, t * P:(t + 1) * P],
                                                                      w2[m][:, i, :], start=(i == 0), stop=(i == HT - 1))
                                    mm.then_inc(out_ready, 1)

                        @block.scalar
                        def _(act):
                            for s, (m, c) in enumerate(STEPS):
                                if s >= 2:
                                    act.wait_ge(out_ready, s - 1)
                                for i in range(HT):
                                    act.wait_ge(hid_ready, HT * s + i + 1)
                                    nc.scalar.activation(hid[:, s % 2, i, :], ps_h[:, i, :], ACT.Gelu,
                                                         bias=b1[:, m, i:i + 1]).then_inc(gelu_done, 1)

                        @block.vector
                        def _(dve):
                            n = [0]

                            def link(ins):
                                n[0] += 1
                                ins.then_inc(step, 1)
                                dve.wait_ge(step, n[0])

                            for s, (m, c) in enumerate(STEPS):
                                dve.wait_ge(out_ready, s + 1)
                                o = ps_o[:, s % 2, :]
                                if m < 2:
                                    link(nc.vector.tensor_scalar(rest[:, 0], o, b2[:, m:m + 1], (SCALE, 1.0)[m],
                                                                 ALU.add, ALU.mult))
                                    for j in range(SPLITS):
                                        part = parts[:, m, j, c * 512:(c + 1) * 512]
                                        ins = nc.vector.tensor_copy(part, rest[:, j])
                                        if j < SPLITS - 1:
                                            link(ins)
                                            link(nc.vector.tensor_tensor(rest[:, j + 1], rest[:, j], part, ALU.subtract))
                                    ins.then_inc(out_read, 1)
                                else:
                                    nc.vector.tensor_tensor(
                                        va[:, 4 * c:4 * c + 4, :, 0:DH0], o.rearrange("p (t h d) -> p t h d", t=4, d=DH0),
                                        b2v[:].rearrange("p (h d) -> p h d", d=DH0).unsqueeze(1)
                                        .to_broadcast([P, 4, H, DH0]), ALU.add).then_inc(out_read, 1)

                with ExitStack() as ctx:
                    va_cur = sb("va_cur", [P, NT, 32], ctx=ctx)
                    pt = sb("pt", [P, NT, 512], ctx=ctx)
                    mx = sb("mx", [P, NT], ctx=ctx)
                    nm = sb("nm", [NT, 2, P], BF16, ctx=ctx)
                    nm32 = sb("nm32", [NT, P], ctx=ctx)
                    ot_sb = sb("ot_sb", [P, 512], ctx=ctx)
                    rec = sb("rec", [P, 4], ctx=ctx)
                    sm = ps("sm", [P, 2, N], ctx)
                    st = ps("st", [P, 2, 512], ctx)
                    ot = ps("ot", [P, 512], ctx)
                    misc = ps("misc", [P, 512], ctx)
                    (sm_ready, sm_free, st_ready, st_free, maxes_ready, turn_ready, misc_free, negmax_part, negmax_ready, negmax_in,
                     va_ready, pv_ready, ot_copied, nat_ready, rec_ready, zeroed, gate) = fresh(
                        ctx, "sm_ready", "sm_free", "st_ready", "st_free", "maxes_ready", "turn_ready", "misc_free",
                        "negmax_part", "negmax_ready", "negmax_in", "va_ready", "pv_ready", "ot_copied", "nat_ready",
                        "rec_ready", "zeroed", "gate")
                    QC = N // 512
                    MAX_AT = (0, 2, 4, 6, 8, 10, 12, 13)

                    with nc.Block() as block:
                        @block.sync
                        def _(sp):
                            def negmax(h):
                                sp.wait_ge(negmax_ready, h + 1)
                                for r in range(2):
                                    sp.dma_start(qsp[KR + r:KR + r + 1, bass.ds(h, 1), :]
                                                 .rearrange("r o (t q) -> r (o t) q", q=P),
                                                 nm[:, r]).then_inc(negmax_in, 16)

                            negmax(0)
                            with sp.Fori(0, H - 1) as h:
                                negmax(h + 1)

                        @block.gpsimd
                        def _(pool):
                            nc.gpsimd.memset(va_cur[:], 0.0).then_inc(zeroed, 1)
                            pool.wait_ge(zeroed, 1)
                            with pool.Fori(0, H) as h:
                                pool.wait_ge(pv_ready, h * (2 * QC))
                                pool.sem_inc(gate, 1)
                                nc.gpsimd.tensor_copy(va_cur[:, :, 0:DH0 + 1],
                                                      va[:, :, bass.ds(h, 1), :]).then_inc(va_ready, 1)

                        @block.tensor
                        def _(pe):
                            def score_max(h, qt):
                                pe.wait_ge(sm_free, h * NT + qt + 1)
                                for kc in range(QC):
                                    mm = nc.tensor.matmul(sm[:, qt % 2, kc * 512:(kc + 1) * 512],
                                                          qsp[0:KR, bass.ds(h, 1), qt * P:(qt + 1) * P],
                                                          ksp[0:KR, bass.ds(h, 1), kc * 512:(kc + 1) * 512],
                                                          start=True, stop=True)
                                mm.then_inc(sm_ready, 1)

                            def turn_max(h, use):
                                pe.wait_ge(maxes_ready, h + 1)
                                pe.wait_ge(misc_free, use)
                                nc.tensor.transpose(misc[0:NT, 0:P], mx[:], ident[:]).then_inc(turn_ready, 1)

                            def score(h, qc, kt):
                                pe.wait_ge(st_free, (h * QC + qc) * NT + kt + 1)
                                if qc == 0 and kt == 0:
                                    pe.wait_ge(negmax_in, 32 * (h + 1))
                                nc.tensor.matmul(st[:, kt % 2, :], ksp[:, bass.ds(h, 1), kt * P:(kt + 1) * P],
                                                 qsp[:, bass.ds(h, 1), qc * 512:(qc + 1) * 512],
                                                 start=True, stop=True).then_inc(st_ready, 1)

                            def weigh(h, qc, half):
                                if half == 0:
                                    if qc == 0:
                                        pe.wait_ge(va_ready, h + 1)
                                    pe.wait_ge(ot_copied, h * QC + qc)
                                pe.wait_ge(st_free, 2 + (h * QC + qc) * NT + 4 * half + 4)
                                for c in range(4):
                                    mm = nc.tensor.matmul(ot[32 * c:32 * c + 32, :], va_cur[:, 4 * half + c, :],
                                                          pt[:, 4 * half + c, :], start=(half == 0), stop=(half == 1))
                                mm.then_inc(pv_ready, 1)

                            def natural(h, qc, use):
                                pe.wait_ge(ot_copied, h * QC + qc + 1)
                                pe.wait_ge(misc_free, use)
                                for j in range(4):
                                    mm = nc.tensor.matmul(misc[:, 16 * j:16 * j + DH0 + 1], ot_sb[:, j * P:(j + 1) * P],
                                                          d32[:, 0:DH0 + 1], start=True, stop=True)
                                mm.then_inc(nat_ready, 1)

                            def head(h, ahead):
                                for qc in range(QC):
                                    for kt in range(NT):
                                        score(h, qc, kt)
                                        if ahead and qc * NT + kt in MAX_AT:
                                            score_max(h + 1, MAX_AT.index(qc * NT + kt))
                                        if qc == 1 and kt == 1:
                                            weigh(h, 0, 1)
                                        if qc == 1 and kt == 3:
                                            natural(h, 0, 3 * h + 2)
                                        if kt == 5:
                                            weigh(h, qc, 0)
                                if ahead:
                                    turn_max(h + 1, 3 * h + 3)
                                weigh(h, 1, 1)
                                natural(h, 1, 3 * h + 3 + ahead)

                            for qt in range(NT):
                                score_max(0, qt)
                            turn_max(0, 1)
                            with pe.Fori(0, H - 1) as h:
                                head(h, 1)
                            head(H - 1, 0)

                        @block.scalar
                        def _(act):
                            def exps(u, first):
                                for kt in range(NT):
                                    act.wait_ge(st_ready, u * NT + kt + 1)
                                    if kt % 4 == 0 and not first:
                                        act.wait_ge(pv_ready, u * 2 - 1 + kt // 4)
                                    nc.scalar.activation(pt[:, kt, :], st[:, kt % 2, :], ACT.Exp).then_inc(st_free, 1)

                            exps(0, True)
                            with act.Fori(1, H * QC) as u:
                                exps(u, False)

                        @block.vector
                        def _(dve):
                            dve.sem_inc(sm_free, 2)
                            dve.sem_inc(st_free, 2)
                            dve.sem_inc(misc_free, 1)

                            def row_max(h, qt):
                                dve.wait_ge(sm_ready, h * NT + qt + 1)
                                ins = nc.vector.reduce_max(mx[:, qt:qt + 1], sm[:, qt % 2, :], AX_X)
                                ins.then_inc(sm_free, 1)

                            def negate(h):
                                dve.wait_ge(turn_ready, h + 1)
                                nc.vector.tensor_scalar(nm32[:], misc[0:NT, 0:P], -1.0, None,
                                                        ALU.mult).then_inc(negmax_part, 1)
                                dve.wait_ge(negmax_part, 2 * h + 1)
                                dve.sem_inc(misc_free, 1)
                                nc.vector.tensor_copy(nm[:, 0], nm32[:]).then_inc(negmax_part, 1)
                                dve.wait_ge(negmax_part, 2 * h + 2)
                                nc.vector.tensor_tensor(nm[:, 1], nm32[:], nm[:, 0],
                                                        ALU.subtract).then_inc(negmax_ready, 1)

                            def copy_sums(h, qc):
                                dve.wait_ge(pv_ready, (h * QC + qc) * 2 + 2)
                                nc.vector.tensor_copy(ot_sb[:], ot[:]).then_inc(ot_copied, 1)

                            def normalise(h, qc):
                                dve.wait_ge(nat_ready, h * QC + qc + 1)
                                m = misc[:, 0:64].rearrange("p (j c) -> p j c", c=16)
                                nc.vector.reciprocal(rec[:], m[:, :, DH0]).then_inc(rec_ready, 1)
                                dve.wait_ge(rec_ready, h * QC + qc + 1)
                                nc.vector.tensor_tensor(ao[:, 4 * qc:4 * qc + 4, bass.ds(h * DH0, DH0)], m[:, :, 0:DH0],
                                                        rec[:].unsqueeze(2).to_broadcast([P, 4, DH0]),
                                                        ALU.mult).then_inc(misc_free, 1)

                            def head(h, ahead):
                                for qt in range(NT):
                                    if ahead:
                                        row_max(h + 1, qt)
                                    if qt == 4:
                                        copy_sums(h, 0)
                                    if qt == 5:
                                        normalise(h, 0)
                                if ahead:
                                    dve.wait_ge(sm_free, 2 + (h + 1) * NT + NT)
                                    dve.sem_inc(maxes_ready, 1)
                                    negate(h + 1)
                                copy_sums(h, 1)
                                normalise(h, 1)

                            for qt in range(NT):
                                row_max(0, qt)
                            dve.wait_ge(sm_free, 2 + NT)
                            dve.sem_inc(maxes_ready, 1)
                            negate(0)
                            with dve.Fori(0, H - 1) as h:
                                head(h, 1)
                            head(H - 1, 0)
            xb = sb("xb", [P, NT, D], ctx=per_batch)
            g1 = sb("g1", [P, NT, D], ctx=per_batch)
            xnT = sb("xnT", [P, KW], ctx=per_batch)
            qT = sb("qT", [P, PAIRS, N], ctx=per_batch)
            kT = sb("kT", [P, PAIRS, KW], ctx=per_batch)
            VB = 1 + (N - DH1 + P - 1) // P
            vn = sb("vn", [P, VB, HW], ctx=per_batch)
            rows_of = [MEM + DH1] + [min(P, N - DH1 - P * k) for k in range(VB - 1)]
            first_of = [0] + [MEM + DH1 + P * k for k in range(VB - 1)]

            with ExitStack() as ctx:
                pw = sb("pw", [P, D], ctx=ctx)
                pb = sb("pb", [P, D], ctx=ctx)
                g0 = sb("g0", [P, NT, D], ctx=ctx)
                gwT = sb("gwT", [P, E], ctx=ctx)
                dw = sb("dw", [P, HT, D], ctx=ctx)
                uw = sb("uw", [P, E, BN], ctx=ctx)
                db = sb("db", [P, HT], ctx=ctx)
                ub = sb("ub", [E, D], ctx=ctx)
                aoT = sb("aoT", [P, N], ctx=ctx)
                dwT = sb("dwT", [P, HT, P], ctx=ctx)
                uwT = sb("uwT", [P, HT, D], ctx=ctx)
                hg = sb("hg", [P, HT, N], ctx=ctx)
                xn = sb("xn1", [P, NT, D], ctx=ctx)
                stats = sb("stats1", [P, NT, 6], ctx=ctx)
                mv = sb("mv1", [P, NT, 2], ctx=ctx)
                std = sb("std1", [P, NT], ctx=ctx)
                rstd = sb("rstd1", [P, NT], ctx=ctx)
                pooled = sb("pooled", [P, 1], ctx=ctx)
                rt = sb("rt", [1, 16, E], ctx=ctx)
                wcol = sb("wcol", [P, HT], ctx=ctx)
                wrow = sb("wrow", [E, P], ctx=ctx)
                idx = sb("idx", [1, E], I32, ctx=ctx)
                pa = ps("pa1", [P, 2, 512], ctx)
                pp = ps("pp1", [P, 2, 512], ctx)
                pf = ps("pf1", [P, 2, 512], ctx)
                pr = ps("pr1", [P, 512], ctx)
                (in_p, turned, copied, proj_ready, dsteps, std_in, std_out, xn_ready, pooled_ready, logits_ready,
                 route_exp, route_in, route_ready, bcast_ready, wcol_ready, hid_ready, hid_done, f_ready, f_done,
                 idx_ready, zeros_set) = fresh(
                    ctx, "in_p", "turned1", "copied1", "proj_ready", "dsteps", "std_in", "std_out", "xn1_ready",
                    "pooled_ready", "logits_ready", "route_exp", "route_in", "route_ready", "bcast_ready", "wcol_ready",
                    "hid1_ready", "hid1_done", "f_ready", "f_done", "idx_ready", "zeros_set")
                with nc.Block() as block:
                    @block.sync
                    def _(sp):
                        with nc.allow_non_contiguous_dma("small weights"):
                            for dst, src in (
                                    (pw[:], A["L0_attn_proj_w"]), (pb[:], A["L0_attn_proj_b"].partition_broadcast(P)),
                                    (g0[:], g0_dram[:, bass.ds(batch * NT, NT), :]),
                                    (xb[:], A["L0_attn_x"].rearrange("b (t p) d -> p (b t) d", p=P)
                                     [:, bass.ds(batch * NT, NT), :]),
                                    (gwT[:], A["L1_ffn_gate_w"].rearrange("e d -> d e")),
                                    (dw[:], A["L1_ffn_down_w"].rearrange("e c d -> (e c) d")
                                     .rearrange("(m p) d -> p m d", p=P)),
                                    (uw[:], A["L1_ffn_up_w"].rearrange("e d c -> d e c")),
                                    (db[:], A["L1_ffn_down_b"].rearrange("e c -> (e c)")
                                     .rearrange("(m p) -> p m", p=P)),
                                    (ub[:], A["L1_ffn_up_b"])):
                                sp.dma_start(dst, src).then_inc(in_p, 16)
                    IN_P = 16 * 9

                    @block.gpsimd
                    def _(pool):
                        nc.gpsimd.memset(xnT[:, 0:MEM], 0.0).then_inc(zeros_set, 1)
                        nc.gpsimd.iota(idx[:], [[-1, E]], base=E, channel_multiplier=0).then_inc(idx_ready, 1)

                    @block.tensor
                    def _(pe):
                        for q in range(2):
                            for t in range(4 * q, 4 * q + 4):
                                mm = nc.tensor.transpose(pa[:, q, (t % 4) * P:(t % 4 + 1) * P], ao[:, t, :], ident[:])
                            mm.then_inc(turned, 1)
                        pe.wait_ge(in_p, IN_P)
                        for q in range(2):
                            pe.wait_ge(copied, q + 1)
                            for t in range(4 * q, 4 * q + 4):
                                mm = nc.tensor.matmul(pp[:, q, (t % 4) * P:(t % 4 + 1) * P], aoT[:, t * P:(t + 1) * P],
                                                      pw[:], start=True, stop=True)
                            mm.then_inc(proj_ready, 1)
                        for q, w in enumerate((dw[:], uw[:].rearrange("p e c -> p (e c)")
                                               .rearrange("p (m c) -> p m c", c=P))):
                            for m in range(HT):
                                mm = nc.tensor.transpose(pa[:, q, m * P:(m + 1) * P], w[:, m, :], ident[:])
                            mm.then_inc(turned, 1)
                        for q in range(2):
                            pe.wait_ge(copied, q + 3)
                            pe.wait_ge(xn_ready, q + 1)
                            for t in range(4 * q, 4 * q + 4):
                                mm = nc.tensor.transpose(pa[:, q, (t % 4) * P:(t % 4 + 1) * P], xn[:, t, :], ident[:])
                            mm.then_inc(turned, 1)
                        pe.wait_ge(pooled_ready, 1)
                        nc.tensor.matmul(pr[0:1, 0:E], pooled[:], gwT[:], start=True, stop=True).then_inc(logits_ready, 1)
                        for c in range(2):
                            for m in range(HT):
                                k = c * HT + m
                                if k >= 2:
                                    pe.wait_ge(hid_done, k - 1)
                                nc.tensor.matmul(pf[:, k % 2, :], dwT[:, m, :], xnT[:, MEM + c * 512:MEM + (c + 1) * 512],
                                                 start=True, stop=True).then_inc(hid_ready, 1)
                        pe.wait_ge(route_ready, 1)
                        nc.tensor.matmul(pr[:, 16:16 + E], ones1[0:1, :], rt[0:1, 15, :], start=True, stop=True)
                        nc.tensor.matmul(pr[0:E, 128:256], rt[0:1, 15, :], ones1[0:1, :], start=True, stop=True
                                         ).then_inc(bcast_ready, 1)
                        pe.wait_ge(wcol_ready, 1)
                        pe.wait_ge(hid_done, 2 * HT)
                        for q in range(2):
                            for t in range(4 * q, 4 * q + 4):
                                o = pf[:, q, (t % 4) * P:(t % 4 + 1) * P]
                                for m in range(HT):
                                    nc.tensor.matmul(o, hg[:, m, t * P:(t + 1) * P], uwT[:, m, :],
                                                     start=(m == 0), stop=False)
                                mm = nc.tensor.matmul(o, wrow[:], ub[:], start=False, stop=True)
                            mm.then_inc(f_ready, 1)

                    @block.scalar
                    def _(act):
                        for q in range(2):
                            act.wait_ge(turned, q + 1)
                            nc.scalar.copy(aoT[:, q * 512:(q + 1) * 512], pa[:, q, :]).then_inc(copied, 1)
                        for q, dst in enumerate((dwT, uwT)):
                            act.wait_ge(turned, q + 3)
                            nc.scalar.copy(dst[:], pa[:, q, :]).then_inc(copied, 1)
                        act.wait_ge(std_in, 1)
                        nc.scalar.activation(std[:], mv[:, :, 1], ACT.Sqrt).then_inc(std_out, 1)
                        for q in range(2):
                            act.wait_ge(turned, q + 5)
                            nc.scalar.copy(xnT[:, MEM + q * 512:MEM + (q + 1) * 512], pa[:, q, :]).then_inc(copied, 1)
                        act.wait_ge(route_in, 1)
                        nc.scalar.activation(rt[0:1, 2, :], rt[0:1, 0, :], ACT.Exp, bias=rt[0:1, 1, 0:1]
                                             ).then_inc(route_exp, 1)
                        for c in range(2):
                            for m in range(HT):
                                k = c * HT + m
                                act.wait_ge(hid_ready, k + 1)
                                nc.scalar.activation(hg[:, m, c * 512:(c + 1) * 512], pf[:, k % 2, :], ACT.Gelu,
                                                     bias=db[:, m:m + 1]).then_inc(hid_done, 1)
                        for q in range(2):
                            act.wait_ge(f_ready, q + 1)
                            nc.scalar.activation(g1[:, 4 * q:4 * q + 4, :], pf[:, q, :], ACT.Silu).then_inc(f_done, 1)

                    @block.vector
                    def _(dve):
                        n = [0]

                        def link(ins):
                            n[0] += 1
                            ins.then_inc(dsteps, 1)
                            dve.wait_ge(dsteps, n[0])

                        dve.wait_ge(in_p, IN_P)
                        for q in range(2):
                            dve.wait_ge(proj_ready, q + 1)
                            half = slice(4 * q, 4 * q + 4)
                            link(nc.vector.tensor_tensor(xn[:, half, :], pp[:, q, :].rearrange("p (t d) -> p t d", d=D),
                                                         pb[:].unsqueeze(1).to_broadcast([P, 4, D]), ALU.add))
                            link(nc.vector.tensor_tensor(xn[:, half, :], xn[:, half, :], g0[:, half, :], ALU.mult))
                            link(nc.vector.tensor_tensor(xb[:, half, :], xb[:, half, :], xn[:, half, :], ALU.add))
                        for t in range(NT):
                            ins = nc.vector.bn_stats(stats[:, t, :], xb[:, t, :])
                        link(ins)
                        for t in range(NT):
                            ins = nc.vector.bn_aggr(mv[:, t, :], stats[:, t, :])
                        link(ins)
                        nc.vector.tensor_scalar_add(mv[:, :, 1], mv[:, :, 1], 1e-5).then_inc(std_in, 1)
                        dve.wait_ge(std_out, 1)
                        link(nc.vector.reciprocal(rstd[:], std[:]))
                        for t in range(NT):
                            ins = nc.vector.tensor_scalar(xn[:, t, :], xb[:, t, :], mv[:, t, 0:1], rstd[:, t:t + 1],
                                                          ALU.subtract, ALU.mult)
                            if t % 4 == 3:
                                ins.then_inc(xn_ready, 1)
                        dve.wait_ge(copied, 6)
                        link(nc.vector.reduce_sum(pooled[:], xnT[:, MEM:KW], AX_X))
                        nc.vector.tensor_scalar(pooled[:], pooled[:], 1.0 / N, None, ALU.mult).then_inc(pooled_ready, 1)
                        dve.wait_ge(idx_ready, 1)
                        order = rt[0:1, 3, :]
                        link(nc.vector.tensor_copy(order, idx[:]))
                        dve.wait_ge(logits_ready, 1)
                        link(nc.vector.tensor_copy(rt[0:1, 0, :], pr[0:1, 0:E]))
                        link(nc.vector.reduce_max(rt[0:1, 1, 1:2], rt[0:1, 0, :], AX_X))
                        nc.vector.tensor_scalar(rt[0:1, 1, 0:1], rt[0:1, 1, 1:2], -1.0, None, ALU.mult
                                                ).then_inc(route_in, 1)
                        dve.wait_ge(route_exp, 1)
                        link(nc.vector.reduce_sum(rt[0:1, 1, 2:3], rt[0:1, 2, :], AX_X))
                        link(nc.vector.reciprocal(rt[0:1, 1, 3:4], rt[0:1, 1, 2:3]))
                        gate = rt[0:1, 4, :]
                        link(nc.vector.tensor_scalar(gate, rt[0:1, 2, :], rt[0:1, 1, 3:4], None, ALU.mult))
                        left, chosen = gate, []
                        for k in range(2):
                            top, pick, key, one, rest_of = (rt[0:1, 5 + 5 * k, k:k + 1], rt[0:1, 6 + 5 * k, 0:1],
                                                            rt[0:1, 7 + 5 * k, :], rt[0:1, 8 + 5 * k, :],
                                                            rt[0:1, 9, :])
                            link(nc.vector.reduce_max(top, left, AX_X))
                            link(nc.vector.tensor_scalar(key, left, top, None, ALU.is_equal))
                            link(nc.vector.tensor_tensor(key, key, order, ALU.mult))
                            link(nc.vector.reduce_max(pick, key, AX_X))
                            link(nc.vector.tensor_scalar(one, key, pick, None, ALU.is_equal))
                            chosen.append(one)
                            if k == 0:
                                link(nc.vector.tensor_scalar(rest_of, one, -2.0, None, ALU.mult))
                                link(nc.vector.tensor_tensor(rest_of, rest_of, gate, ALU.add))
                                left = rest_of
                        link(nc.vector.tensor_tensor(chosen[0], chosen[0], chosen[1], ALU.add))
                        link(nc.vector.tensor_tensor(gate, gate, chosen[0], ALU.mult))
                        link(nc.vector.reduce_sum(rt[0:1, 1, 4:5], gate, AX_X))
                        link(nc.vector.tensor_scalar(rt[0:1, 1, 4:5], rt[0:1, 1, 4:5], 1e-8, None, ALU.add))
                        link(nc.vector.reciprocal(rt[0:1, 1, 5:6], rt[0:1, 1, 4:5]))
                        nc.vector.tensor_scalar(rt[0:1, 15, :], gate, rt[0:1, 1, 5:6], None, ALU.mult
                                                ).then_inc(route_ready, 1)
                        dve.wait_ge(bcast_ready, 1)
                        for e in range(2):
                            link(nc.vector.tensor_copy(wcol[e * BN:(e + 1) * BN, :],
                                                       pr[e * BN:(e + 1) * BN, 16 + e:16 + E:2]))
                        link(nc.vector.tensor_copy(wrow[:], pr[0:E, 128:256]))
                        link(nc.vector.tensor_tensor(uwT[:], uwT[:], wcol[:].unsqueeze(2).to_broadcast([P, HT, D]),
                                                     ALU.mult))
                        dve.sem_inc(wcol_ready, 1)

            with ExitStack() as ctx:
                w3 = [sb(f"w3_{m}", [P, HW], ctx=ctx) for m in "qkv"]
                sq = sb("sq", [P, 2, 512], ctx=ctx)
                nr = sb("nr", [H, 2, 512], ctx=ctx)
                mk = sb("mk", [P, PAIRS, MEM], ctx=ctx)
                mks = sb("mks", [P, PAIRS * MEM], ctx=ctx)
                mkr = sb("mkr", [P, PAIRS * MEM], ctx=ctx)
                pick = sb("pick", [P, PAIRS, H], ctx=ctx)
                spread = sb("spread", [H, PAIRS, P], ctx=ctx)
                pq = ps("pq", [P, 2, 512], ctx)
                pn = ps("pn", [P, 2, 512], ctx)
                pb_ = ps("pspread", [P, 2, 512], ctx)
                pv = ps("pv", [P, 2, 512], ctx)
                (in_q, in_k, in_v, in_m, picks_set, q_ready, sq_ready, copied, sums_done, root_ready, inv_ready, spread_done,
                 scaled, msq, msum, mroot, steps, v_ready, v_done, mem_in) = fresh(
                    ctx, "in_q", "in_k", "in_v", "in_m", "picks_set", "q_ready", "sq_ready", "copied", "sums_done", "root_ready",
                    "inv_ready", "spread_done", "scaled", "msq", "msum", "mroot", "qkv_steps", "v_ready", "v_done",
                    "mem_in")
                UNITS = [(w, c, r) for w in range(2) for c in range(N // 512) for r in range(PAIRS)]
                U = len(UNITS)
                LAG = PAIRS + 2
                QK_SCALE = 10.0
                VS = 2 * VB

                def values_at(u):
                    return range(2 * (u - U), min(2 * (u - U) + 2, VS)) if u >= U else range(0)

                def place(u):
                    w, c, r = UNITS[u]
                    return (qT[:, r, c * 512:(c + 1) * 512], kT[:, r, MEM + c * 512:MEM + (c + 1) * 512])[w]

                with nc.Block() as block:
                    @block.sync
                    def _(sp):
                        for w, name, there in ((0, "L1_attn_Wq", in_q), (1, "L1_attn_Wk", in_k), (2, "L1_attn_Wv", in_v)):
                            sp.dma_start(w3[w][:], A[name]).then_inc(there, 16)
                        with nc.allow_non_contiguous_dma("memory keys to channels on partitions"):
                            mkeys = A["L1_attn_mem_k"].rearrange("(r two) m d -> two d r m", two=2)
                            for two in range(2):
                                for r in range(PAIRS):
                                    sp.dma_start(mk[two * DH1:(two + 1) * DH1, r, :], mkeys[two, :, r, :]
                                                 ).then_inc(in_m, 16)
                        sp.wait_ge(v_done, 2)
                        sp.dma_start(vn[0:MEM, 0, :].rearrange("m (h d) -> m h d", d=DH1),
                                     A["L1_attn_mem_v"].rearrange("h m d -> m h d")).then_inc(mem_in, 16)
                        sp.wait_ge(mem_in, 16)
                    IN_M = 16 * 2 * PAIRS

                    @block.gpsimd
                    def _(pool):
                        nc.gpsimd.memset(pick[:], 0.0).then_inc(picks_set, 1)
                        pool.wait_ge(picks_set, 1)
                        flat = pick[:].rearrange("p r h -> p (r h)")
                        for half in range(2):
                            nc.gpsimd.memset(flat[half * DH1:(half + 1) * DH1, half:PAIRS * H:H + 2], 1.0
                                             ).then_inc(picks_set, 1)
                            pool.wait_ge(picks_set, 2 + half)
                        nc.gpsimd.tensor_copy(spread[:].rearrange("h r (two d) -> h (r two) d", d=DH1),
                                              ident[0:H, 0:H].unsqueeze(2).to_broadcast([H, H, DH1])
                                              ).then_inc(picks_set, 1)

                    @block.tensor
                    def _(pe):
                        for u in range(U + LAG):
                            if u < U:
                                w, c, r = UNITS[u]
                                if u % (U // 2) == 0:
                                    pe.wait_ge((in_q, in_k)[w], 16)
                                if u >= 2:
                                    pe.wait_ge(copied, u - 1)
                                nc.tensor.matmul(pq[:, u % 2, :], w3[w][:, r * P:(r + 1) * P],
                                                 xnT[:, MEM + c * 512:MEM + (c + 1) * 512], start=True, stop=True
                                                 ).then_inc(q_ready, 1)
                            for k in values_at(u):
                                b, c = k // 2, k % 2
                                if k == 0:
                                    pe.wait_ge(in_v, 16)
                                if k >= 2:
                                    pe.wait_ge(v_done, k - 1)
                                nc.tensor.matmul(pv[0:rows_of[b], k % 2, :], xnT[:, first_of[b]:first_of[b] + rows_of[b]],
                                                 w3[2][:, c * 512:(c + 1) * 512], start=True, stop=True
                                                 ).then_inc(v_ready, 1)
                            if 1 <= u <= U:
                                g, r = divmod(u - 1, PAIRS)
                                if u == 1:
                                    pe.wait_ge(picks_set, 4)
                                if r == 0 and g >= 2:
                                    pe.wait_ge(root_ready, g - 1)
                                pe.wait_ge(sq_ready, u)
                                nc.tensor.matmul(pn[0:H, g % 2, :], pick[:, r, :], sq[:, (u - 1) % 2, :],
                                                 start=(r == 0), stop=(r == PAIRS - 1)).then_inc(sums_done, 1)
                            if u >= LAG:
                                g, r = divmod(u - LAG, PAIRS)
                                if r == 0:
                                    pe.wait_ge(inv_ready, g + 1)
                                if u - LAG >= 2:
                                    pe.wait_ge(scaled, u - LAG - 1)
                                nc.tensor.matmul(pb_[:, (u - LAG) % 2, :], spread[:, r, :], nr[:, g % 2, :],
                                                 start=True, stop=True).then_inc(spread_done, 1)
                        pe.wait_ge(msq, 1)
                        nc.tensor.matmul(pn[:, 0, 0:PAIRS * MEM], headones[:], mks[:], start=True, stop=True
                                         ).then_inc(msum, 1)

                    @block.scalar
                    def _(act):
                        for u in range(U + LAG):
                            if u < U:
                                act.wait_ge(copied, u + 1)
                                if u >= 2:
                                    act.wait_ge(sums_done, u - 1)
                                nc.scalar.activation(sq[:, u % 2, :], place(u), ACT.Square).then_inc(sq_ready, 1)
                            if u == 4:
                                act.wait_ge(in_m, IN_M)
                                nc.scalar.activation(mks[:], mk[:].rearrange("p r m -> p (r m)"), ACT.Square
                                                     ).then_inc(msq, 1)
                            if 0 < u <= U and u % PAIRS == 0:
                                g = u // PAIRS - 1
                                act.wait_ge(sums_done, u)
                                if g >= 2:
                                    act.wait_ge(spread_done, (g - 1) * PAIRS)
                                nc.scalar.activation(nr[:, g % 2, :], pn[0:H, g % 2, :], ACT.Sqrt
                                                     ).then_inc(root_ready, 1)
                            for k in values_at(u):
                                b, c = k // 2, k % 2
                                act.wait_ge(v_ready, k + 1)
                                nc.scalar.copy(vn[0:rows_of[b], b, c * 512:(c + 1) * 512], pv[0:rows_of[b], k % 2, :]
                                               ).then_inc(v_done, 1)
                        act.wait_ge(msum, 1)
                        nc.scalar.activation(mkr[:], pn[:, 0, 0:PAIRS * MEM], ACT.Sqrt).then_inc(mroot, 1)

                    @block.vector
                    def _(dve):
                        n = [0]

                        def link(ins):
                            n[0] += 1
                            ins.then_inc(steps, 1)
                            dve.wait_ge(steps, n[0])

                        for u in range(U + LAG):
                            if u < U:
                                dve.wait_ge(q_ready, u + 1)
                                nc.vector.tensor_copy(place(u), pq[:, u % 2, :]).then_inc(copied, 1)
                            if 0 < u <= U and u % PAIRS == 0:
                                g = u // PAIRS - 1
                                root = nr[:, g % 2, :]
                                dve.wait_ge(root_ready, g + 1)
                                link(nc.vector.tensor_scalar(root, root, 1e-12, None, ALU.max))
                                nc.vector.reciprocal(root, root).then_inc(inv_ready, 1)
                            if u >= LAG:
                                dve.wait_ge(copied, u - LAG + 1)
                                dve.wait_ge(spread_done, u - LAG + 1)
                                at = place(u - LAG)
                                nc.vector.scalar_tensor_tensor(at, at, (QK_SCALE, 1.0)[UNITS[u - LAG][0]],
                                                               pb_[:, (u - LAG) % 2, :], ALU.mult, ALU.mult
                                                               ).then_inc(scaled, 1)
                        dve.wait_ge(mroot, 1)
                        link(nc.vector.tensor_scalar(mkr[:], mkr[:], 1e-12, None, ALU.max))
                        link(nc.vector.reciprocal(mkr[:], mkr[:]))
                        nc.vector.tensor_tensor(kT[:, :, 0:MEM], mkr[:].rearrange("p (r m) -> p r m", m=MEM), mk[:],
                                                ALU.mult)

            G = N // DH1
            UT = DH1 // IL
            PQ = UT // 2
            PR = G * PQ
            width = [MEM + DH1 * (s + 1) for s in range(G)]
            COUNTS = 4
            TARGET = TOPK - PICK / 2.0 - 0.25
            FIRST_STEP = 0.8
            SHORTER, LONGER = 0.5, 1.4

            def pieces(s):
                k = -(-width[s] // 512)
                cut = [width[s] * i // k for i in range(k + 1)]
                return list(zip(cut[:-1], cut[1:]))

            def key_blocks(s):
                return [(k, rows_of[k] if k == 0 else min(P, width[s] - first_of[k]))
                        for k in range(VB) if first_of[k] < width[s]]

            def copies_of(s):
                whole = [k for k, rows in key_blocks(s) if rows == P]
                part = [[k] for k, rows in key_blocks(s) if rows != P]
                return part[:1] + [whole[i:i + 4] for i in range(0, len(whole), 4)] + part[1:]

            def before(f, s):
                return sum(UT * f(g) for g in range(s))

            n_pieces = [len(pieces(s)) for s in range(G)]
            n_copies = [len(copies_of(s)) for s in range(G)]

            def pieces_before(t):
                return before(lambda g: n_pieces[g], t // UT) + (t % UT) * n_pieces[min(t // UT, G - 1)]

            def copies_before(t):
                return before(lambda g: n_copies[g], t // UT) + (t % UT) * n_copies[min(t // UT, G - 1)]

            def stream(p):
                return [(j, c) for j in range(2) for c in pieces(p // PQ)]

            def at_least(eng, s, value):
                if not isinstance(value, int) or value > 0:
                    eng.wait_ge(s, value)

            qT_dram = nc.dram_tensor("qT_dram", [P, PAIRS * N], F32, kind="Internal").ap()

            again_row = sb("again_row", [P, 2], ctx=per_batch)
            again_any = sb("again_any", [P, 1], ctx=per_batch)
            again_int = sb("again_int", [P, 1], I32, ctx=per_batch)

            with ExitStack() as ctx:
                aT = sb("aT", [P, VB, UT, P], ctx=ctx)
                qs = sb("qs", [P, 2, 4, 2, 32], ctx=ctx)
                dots = sb("dots", [P, 2, 512], ctx=ctx)
                xs = sb("xs", [P, 3, 2, KW], ctx=ctx)
                wk = sb("wk", [P, 2, KW], ctx=ctx)
                ex = sb("ex", [P, 2, KW], ctx=ctx)
                junk = sb("junk", [P, KW], BF16, ctx=ctx)
                sample = sb("sample", [P, 2, 2, 8], ctx=ctx)
                top = sb("top", [P, 2, 8, 8], ctx=ctx)
                picked = sb("picked", [P, 2, PICK], ctx=ctx)
                rmax = sb("rmax", [P, 3, 2], ctx=ctx)
                nmax = sb("nmax", [P, 3, 2], ctx=ctx)
                bound = sb("bound", [P, 3, 2], ctx=ctx)
                slope = sb("slope", [P, 3, 2], ctx=ctx)
                off = sb("off", [P, 3, 2, 2], ctx=ctx)
                signs = sb("signs", [P, 3, 2], ctx=ctx)
                tmp = sb("tmp", [P, 4, 2], ctx=ctx)
                found = sb("found", [P, 2, 2], ctx=ctx)
                fewest = sb("fewest", [P, 2], ctx=ctx)
                most = sb("most", [P, 2], ctx=ctx)
                outside = sb("outside", [P, 2], ctx=ctx)
                sc = sb("sc", [P, 2, 4], ctx=ctx)
                mix = sb("mix", [P, 2, P], ctx=ctx)
                pa = ps("pa2", [P, 2, 512], ctx)
                pb = ps("pb2", [P, 2, 512], ctx)
                pc = ps("pc2", [P, 2, 512], ctx)
                po = ps("po2", [P, PAIRS, DH1], ctx)
                pf = ps("pf2", [P, 2], ctx)
                (saved, qs_zero, qs_ready, qk_ready, dots_ready, mixed, xs_ready, sampled, start_ready, bound_ready,
                 counted, pool_step, ex_ready, step, p_ready, turned, at_ready, av_ready, av_done, outside_ready,
                 outside_sum) = fresh(
                    ctx, "saved", "qs_zero", "qs_ready", "qk_ready", "dots_ready", "mixed", "xs_ready", "sampled",
                    "start_ready", "bound_ready", "counted", "pool_step", "ex_ready", "dve_chain", "p_ready", "turned2",
                    "at_ready", "av_ready", "av_done", "outside_ready", "outside_sum")
                SOUGHT = range(PQ, PR)

                def every(k):
                    return 2 if k == 0 else 1

                def counts_before(p, k):
                    return (p - PQ) * COUNTS + k

                with nc.Block() as block:
                    @block.sync
                    def _(sp):
                        sp.dma_start(qT_dram, qT[:].rearrange("p r n -> p (r n)")).then_inc(saved, 16)
                        sp.wait_ge(saved, 16)

                    @block.gpsimd
                    def _(pool):
                        n = [0]

                        def link(ins):
                            n[0] += 1
                            ins.then_inc(pool_step, 1)
                            pool.wait_ge(pool_step, n[0])

                        def stage(p, j):
                            if not 0 <= p < PR:
                                return
                            t = 2 * p + j
                            at_least(pool, dots_ready, pieces_before(t - 1) if t >= 2 else 0)
                            for p2 in range(2):
                                for half in range(2):
                                    part = slice(half * DH1, (half + 1) * DH1)
                                    c = (2 * p2 + half) * IL
                                    ins = nc.gpsimd.tensor_copy(qs[part, j, :, p2, c:c + IL],
                                                                qT[part, p2:PAIRS:2, t * IL:(t + 1) * IL])
                            ins.then_inc(qs_ready, 1)
                            pool.wait_ge(qs_ready, t + 1)

                        def start(p):
                            if not 0 <= p < PR:
                                return
                            q = p % 3
                            pool.wait_ge(sampled, p + 1)
                            ins = nc.gpsimd.tensor_scalar(nmax[:, q], rmax[:, q], -1.0, None, ALU.mult)
                            if p in SOUGHT:
                                s8 = sample[:, p % 2]
                                nc.gpsimd.tensor_copy(bound[:, q], s8[:, :, 7])
                                link(nc.gpsimd.tensor_tensor(slope[:, q], s8[:, :, 0], s8[:, :, 7], ALU.subtract))
                                ins = nc.gpsimd.tensor_scalar(slope[:, q], slope[:, q], FIRST_STEP, None, ALU.mult)
                            ins.then_inc(start_ready, 1)
                            pool.wait_ge(start_ready, p + 1)

                        def move(p, k):
                            if p not in SOUGHT:
                                return
                            q, w = p % 3, width[p // PQ]
                            new, old = off[:, q, k % 2], off[:, q, (k + 1) % 2]
                            pool.wait_ge(counted, 2 * counts_before(p, k + 1))
                            if k == 0:
                                pool.wait_ge(start_ready, p + 1)
                            scale = -(LONGER - SHORTER) ** k / (32.0 * TARGET * TARGET)
                            a = 10 * TARGET - w
                            m = every(k)
                            nc.gpsimd.tensor_scalar(tmp[:, 0], signs[:, q], (2 * TARGET - w) / m, scale * m * m,
                                                    ALU.add, ALU.mult)
                            link(nc.gpsimd.tensor_scalar(tmp[:, 1], signs[:, q], a / m, 3.2 * TARGET / m,
                                                         ALU.add, ALU.max))
                            link(nc.gpsimd.tensor_tensor(new, tmp[:, 0], tmp[:, 1], ALU.mult))
                            if k > 0:
                                link(nc.gpsimd.tensor_tensor(tmp[:, 2], new, old, ALU.mult))
                                link(nc.gpsimd.tensor_scalar(tmp[:, 2], tmp[:, 2], 0.0, SHORTER / (LONGER - SHORTER),
                                                             ALU.is_gt, ALU.add))
                                link(nc.gpsimd.tensor_tensor(slope[:, q], slope[:, q], tmp[:, 2], ALU.mult))
                            link(nc.gpsimd.tensor_tensor(tmp[:, 3], new, slope[:, q], ALU.mult))
                            nc.gpsimd.tensor_tensor(bound[:, q], bound[:, q], tmp[:, 3], ALU.add
                                                    ).then_inc(bound_ready, 1)
                            pool.wait_ge(bound_ready, counts_before(p, k + 1))

                        nc.gpsimd.memset(qs[:], 0.0).then_inc(qs_zero, 1)
                        pool.wait_ge(qs_zero, 1)
                        for j in range(2):
                            stage(0, j)
                        for p in range(-2, PR):
                            move(p + 1, 1)
                            stage(p + 3, 0)
                            move(p + 1, 2)
                            stage(p + 3, 1)
                            start(p + 2)
                            move(p + 1, 3)
                            move(p + 2, 0)

                    @block.tensor
                    def _(pe):
                        def front(p, steps):
                            if not 0 <= p < PR:
                                return
                            todo = stream(p)
                            at = pieces_before(2 * p)
                            for n in steps:
                                if n < len(todo):
                                    j, (c0, c1) = todo[n]
                                    b = (at + n) % 2
                                    pe.wait_ge(qs_ready, 2 * p + j + 1)
                                    at_least(pe, dots_ready, at + n - 1)
                                    for p2 in range(2):
                                        for cg in range(4):
                                            mm = nc.tensor.matmul(pa[32 * cg:32 * cg + 32, b, 0:c1 - c0],
                                                                  qs[:, j, cg, p2, :], kT[:, 2 * cg + p2, c0:c1],
                                                                  start=(p2 == 0), stop=(p2 == 1))
                                    mm.then_inc(qk_ready, 1)
                                if 1 <= n <= len(todo):
                                    j, (c0, c1) = todo[n - 1]
                                    b = (at + n - 1) % 2
                                    pe.wait_ge(dots_ready, at + n)
                                    at_least(pe, xs_ready, at + n - 2)
                                    nc.tensor.matmul(pb[:, b, 0:c1 - c0], kron_pre[:].rearrange("p h i -> p (h i)"),
                                                     dots[:, b, 0:c1 - c0], start=True, stop=True).then_inc(mixed, 1)

                        def back(p, j):
                            if p < 0:
                                return
                            s = p // PQ
                            at = copies_before(2 * p + j)
                            pe.wait_ge(p_ready, 2 * p + j + 1)
                            for n, ks in enumerate(copies_of(s)):
                                b = (at + n) % 2
                                at_least(pe, at_ready, at + n - 1)
                                for m, kb in enumerate(ks):
                                    rows = dict(key_blocks(s))[kb]
                                    mm = nc.tensor.matmul(pc[0:rows, b, m * P:(m + 1) * P],
                                                          ex[:, j, first_of[kb]:first_of[kb] + rows], mix[:, j, :],
                                                          start=True, stop=True)
                                mm.then_inc(turned, 1)

                        def weigh(s):
                            pe.wait_ge(at_ready, before(lambda g: n_copies[g], s + 1))
                            at_least(pe, av_done, s)
                            blocks = key_blocks(s)
                            for r in range(PAIRS):
                                for k, rows in blocks:
                                    for half in range(2):
                                        h = 2 * r + half
                                        mm = nc.tensor.matmul(
                                            po[half * DH1:(half + 1) * DH1, r, :], vn[0:rows, k, h * DH1:(h + 1) * DH1],
                                            aT[0:rows, k, :, h * IL:(h + 1) * IL],
                                            start=(k == 0), stop=(k == blocks[-1][0]))
                            mm.then_inc(av_ready, 1)

                        for p in range(-2, PR + 1):
                            front(p + 2, (0,))
                            front(p + 2, (1,))
                            back(p - 1, 0)
                            front(p + 2, (2,))
                            front(p + 2, (3,))
                            front(p + 2, (4, 5, 6))
                            back(p - 1, 1)
                            if p > 0 and p % PQ == 0:
                                weigh(p // PQ - 1)
                        pe.wait_ge(outside_ready, 1)
                        nc.tensor.matmul(pf[:], ones1[:], outside[:], start=True, stop=True).then_inc(outside_sum, 1)

                    @block.scalar
                    def _(act):
                        def front(p, steps):
                            if not 0 <= p < PR:
                                return
                            todo = stream(p)
                            at = pieces_before(2 * p)
                            for n in steps:
                                if n < len(todo):
                                    j, (c0, c1) = todo[n]
                                    b = (at + n) % 2
                                    act.wait_ge(qk_ready, at + n + 1)
                                    at_least(act, mixed, at + n - 1)
                                    nc.scalar.copy(dots[:, b, 0:c1 - c0], pa[:, b, 0:c1 - c0]).then_inc(dots_ready, 1)
                                if 1 <= n <= len(todo):
                                    j, (c0, c1) = todo[n - 1]
                                    b = (at + n - 1) % 2
                                    at_least(act, p_ready, 2 * p + j - 5)
                                    act.wait_ge(mixed, at + n)
                                    nc.scalar.copy(xs[:, p % 3, j, c0:c1], pb[:, b, 0:c1 - c0]).then_inc(xs_ready, 1)

                        def count(p, k):
                            if p not in SOUGHT:
                                return
                            q, w = p % 3, width[p // PQ]
                            if k == 0:
                                act.wait_ge(start_ready, p + 1)
                            else:
                                act.wait_ge(bound_ready, counts_before(p, k))
                            for j in range(2):
                                at_least(act, counted, 2 * counts_before(p, k) + j)
                                m = every(k)
                                nc.scalar.activation(junk[:, 0:w // m], xs[:, q, j, 0:w:m], ACT.Sign, scale=-1.0,
                                                     bias=bound[:, q, j:j + 1], accum_out=signs[:, q, j:j + 1]
                                                     ).then_inc(counted, 1)

                        def exps(p, j):
                            if not 0 <= p < PR:
                                return
                            w = width[p // PQ]
                            act.wait_ge(start_ready, p + 1)
                            at_least(act, turned, copies_before(2 * (p - 1) + j + 1) if p > 0 else 0)
                            nc.scalar.activation(ex[:, j, 0:w], xs[:, p % 3, j, 0:w], ACT.Exp,
                                                 bias=nmax[:, p % 3, j:j + 1]).then_inc(ex_ready, 1)

                        def back(p, j):
                            if p < 0:
                                return
                            t = 2 * p + j
                            at = copies_before(t)
                            for n, ks in enumerate(copies_of(p // PQ)):
                                b = (at + n) % 2
                                rows = dict(key_blocks(p // PQ))[ks[0]]
                                act.wait_ge(turned, at + n + 1)
                                nc.scalar.copy(aT[0:rows, ks[0]:ks[-1] + 1, t % UT, :],
                                               pc[0:rows, b, 0:len(ks) * P].rearrange("p (k c) -> p k c", c=P)
                                               ).then_inc(at_ready, 1)

                        for p in range(-2, PR + 1):
                            front(p + 2, (0,))
                            count(p + 1, 1)
                            front(p + 2, (1,))
                            back(p - 1, 0)
                            exps(p, 0)
                            front(p + 2, (2,))
                            count(p + 1, 2)
                            front(p + 2, (3,))
                            front(p + 2, (4, 5, 6))
                            back(p - 1, 1)
                            exps(p, 1)
                            count(p + 1, 3)
                            if p > 0 and p % PQ == 0:
                                s = p // PQ - 1
                                act.wait_ge(av_ready, s + 1)
                                if s == 0:
                                    act.wait_ge(saved, 16)
                                nc.scalar.copy(qT[:, :, s * DH1:(s + 1) * DH1], po[:]).then_inc(av_done, 1)
                            count(p + 2, 0)

                    @block.vector
                    def _(dve):
                        n = [0]

                        def do(ins):
                            n[0] += 1
                            return ins.then_inc(step, 1)

                        def last(back=0):
                            dve.wait_ge(step, n[0] - back)

                        def prepare(p):
                            if not 0 <= p < PR:
                                return
                            q, w = p % 3, width[p // PQ]
                            for j in range(2):
                                t = 2 * p + j
                                dve.wait_ge(xs_ready, pieces_before(t + 1))
                                at = (UT - 1) * IL - (t % UT) * IL
                                do(nc.vector.tensor_tensor(xs[:, q, j, w - DH1:w], xs[:, q, j, w - DH1:w],
                                                           slide[:, at:at + DH1], ALU.add))
                            for j in range(2):
                                last(1 - j)
                                ins = nc.vector.reduce_max(rmax[:, q, j:j + 1], xs[:, q, j, 0:w], AX_X)
                                if p in SOUGHT:
                                    ins = nc.vector.max(sample[:, p % 2, j, :], xs[:, q, j, 0:w:8])
                            ins.then_inc(sampled, 1)

                        def rounds(src, count, p):
                            for r in range(count):
                                if r == count - 1:
                                    prepare(p)
                                for j in range(2):
                                    last(1)
                                    do(nc.vector.max(top[:, j, r, :], src[j] if r == 0 else wk_of[j]))
                                if r < count - 1:
                                    for j in range(2):
                                        last(1)
                                        do(nc.vector.match_replace(wk_of[j], top[:, j, r, :],
                                                                   src[j] if r == 0 else wk_of[j], -BIG))

                        do(nc.vector.memset(fewest[:], TARGET))
                        do(nc.vector.memset(most[:], TARGET))
                        prepare(0)
                        prepare(1)
                        for p in range(PR):
                            q, w = p % 3, width[p // PQ]
                            x = [xs[:, q, j, 0:w] for j in range(2)]
                            wk_of = [wk[:, j, 0:w] for j in range(2)]
                            if p not in SOUGHT:
                                dve.wait_ge(step, n[0])
                                rounds(x, TOPK // 8, p + 2)
                                kept = [top[:, j, 7, 7:8] for j in range(2)]
                            else:
                                dve.wait_ge(bound_ready, counts_before(p, COUNTS))
                                dve.wait_ge(step, n[0])
                                for j in range(2):
                                    do(nc.vector.tensor_scalar(wk_of[j], x[j], bound[:, q, j:j + 1], None, ALU.is_ge,
                                                               ALU.add, accum_out=found[:, p % 2, j:j + 1]))
                                for j in range(2):
                                    last(1)
                                    do(nc.vector.scalar_tensor_tensor(wk_of[j], wk_of[j], -BIG, x[j], ALU.mult, ALU.add))
                                rounds(wk_of, ROUNDS, p + 2)
                                for j in range(2):
                                    last(1)
                                    do(nc.vector.scalar_tensor_tensor(
                                        picked[:, j, :], ranks[:], found[:, p % 2, j:j + 1],
                                        top[:, j, 0:ROUNDS, :].rearrange("p r e -> p (r e)"), ALU.is_equal, ALU.mult,
                                        accum_out=sc[:, j, 0:1]))
                                nc.vector.tensor_tensor(fewest[:], fewest[:], found[:, p % 2], ALU.min)
                                do(nc.vector.tensor_tensor(most[:], most[:], found[:, p % 2], ALU.max))
                                kept = [sc[:, j, 0:1] for j in range(2)]
                            for j in range(2):
                                dve.wait_ge(ex_ready, 2 * p + j + 1)
                                dve.wait_ge(step, n[0] - (2 - j if p in SOUGHT else 0))
                                nc.vector.scalar_tensor_tensor(ex[:, j, 0:w], x[j], kept[j], ex[:, j, 0:w],
                                                               ALU.is_ge, ALU.mult, accum_out=sc[:, j, 1:2]
                                                               ).then_inc(step, 1)
                                n[0] += 1
                            for j in range(2):
                                last(1)
                                do(nc.vector.reciprocal(sc[:, j, 2:3], sc[:, j, 1:2]))
                            for j in range(2):
                                last(1 - j)
                                nc.vector.tensor_scalar(mix[:, j, :], kron_post[:].rearrange("p h i -> p (h i)"),
                                                        sc[:, j, 2:3], None, ALU.mult).then_inc(p_ready, 1)
                        last()
                        do(nc.vector.tensor_scalar(fewest[:], fewest[:], float(TOPK - PICK), None, ALU.is_lt))
                        do(nc.vector.tensor_scalar(most[:], most[:], float(TOPK - 1), None, ALU.is_gt))
                        last()
                        nc.vector.tensor_tensor(outside[:], fewest[:], most[:], ALU.add).then_inc(outside_ready, 1)
                        dve.wait_ge(outside_sum, 1)
                        do(nc.vector.tensor_scalar(again_row[:], pf[:], 0.0, None, ALU.is_gt))
                        last()
                        do(nc.vector.reduce_max(again_any[:], again_row[:], AX_X))
                        last()
                        do(nc.vector.tensor_copy(again_int[:], again_any[:]))
                        last()

            again = nc.values_load(again_int[0:1, 0:1], min_val=0, max_val=1)

            with ExitStack() as ctx:
                aT = sb("again_aT", [P, VB, UT, P], ctx=ctx)
                qs = sb("again_qs", [P, 2, 4, 2, 32], ctx=ctx)
                dots = sb("again_dots", [P, 2, 512], ctx=ctx)
                xs = sb("again_xs", [P, 2, 2, KW], ctx=ctx)
                wk = sb("again_wk", [P, 2, KW], ctx=ctx)
                ex = sb("again_ex", [P, 2, KW], ctx=ctx)
                top64 = sb("again_top64", [P, 2, 8, 8], ctx=ctx)
                sc = sb("again_sc", [P, 2, 4], ctx=ctx)
                mix = sb("again_mix", [P, 2, P], ctx=ctx)
                pa = ps("again_pa2", [P, 2, 512], ctx)
                pb = ps("again_pb2", [P, 2, 512], ctx)
                pc = ps("again_pc2", [P, 2, 512], ctx)
                po = ps("again_po2", [P, PAIRS, DH1], ctx)
                (qs_zero, qs_ready, qk_ready, dots_ready, mixed, xs_ready, negmax, ex_ready, step, p_ready, turned,
                 at_ready, av_ready, av_done, gate, gate_act, restored) = fresh(
                    ctx, "qs_zero", "qs_ready", "qk_ready", "dots_ready", "mixed", "xs_ready", "negmax", "ex_ready",
                    "dve_chain", "p_ready", "turned2", "at_ready", "av_ready", "av_done", "gate2", "gate_act", "restored")

                with nc.Block() as block:
                    @block.sync
                    def _(sp):
                        with sp.If(again > 0):
                            sp.dma_start(qT[:].rearrange("p r n -> p (r n)"), qT_dram).then_inc(restored, 16)
                            sp.wait_ge(restored, 16)

                    @block.gpsimd
                    def _(pool):
                        with pool.If(again > 0):
                            pool.wait_ge(restored, 16)
                            nc.gpsimd.memset(qs[:], 0.0).then_inc(qs_zero, 1)
                            pool.wait_ge(qs_zero, 1)

                            def stage(s, i, j):
                                k = n_pieces[s]
                                if s == 0:
                                    at_least(pool, dots_ready, (2 * i + j - 1) * k)
                                else:
                                    at = before(lambda g: n_pieces[g], s)
                                    back = k if j == 1 else 0
                                    if isinstance(i, int) and i == 0 and j == 0:
                                        pool.wait_ge(dots_ready, at - n_pieces[s - 1])
                                    else:
                                        pool.wait_ge(dots_ready, at + (2 * i + j - 1) * k)
                                        pool.sem_inc(gate, 1)
                                for p2 in range(2):
                                    for half in range(2):
                                        part = slice(half * DH1, (half + 1) * DH1)
                                        c = (2 * p2 + half) * IL
                                        ins = nc.gpsimd.tensor_copy(
                                            qs[part, j, :, p2, c:c + IL],
                                            qT[part, p2:PAIRS:2, bass.ds(s * DH1 + (2 * i + j) * IL, IL)])
                                ins.then_inc(qs_ready, 1)

                            for s in range(G):
                                if s == 0:
                                    for i in range(PQ):
                                        for j in range(2):
                                            stage(s, i, j)
                                else:
                                    for j in range(2):
                                        stage(s, 0, j)
                                    with pool.Fori(1, PQ) as i:
                                        for j in range(2):
                                            stage(s, i, j)

                    @block.tensor
                    def _(pe):
                        with pe.If(again > 0):
                            def front(s, i, j):
                                k, t = n_pieces[s], 2 * i + j
                                at = before(lambda g: n_pieces[g], s) + t * k
                                pe.wait_ge(qs_ready, s * UT + t + 1)
                                cols = pieces(s)
                                for n in range(k + 1):
                                    if n < k:
                                        c0, c1 = cols[n]
                                        b = (j * k + n) % 2
                                        at_least(pe, dots_ready, at + n - 1)
                                        for p2 in range(2):
                                            for cg in range(4):
                                                mm = nc.tensor.matmul(pa[32 * cg:32 * cg + 32, b, 0:c1 - c0],
                                                                      qs[:, j, cg, p2, :], kT[:, 2 * cg + p2, c0:c1],
                                                                      start=(p2 == 0), stop=(p2 == 1))
                                        mm.then_inc(qk_ready, 1)
                                    if n >= 1:
                                        c0, c1 = cols[n - 1]
                                        b = (j * k + n - 1) % 2
                                        pe.wait_ge(dots_ready, at + n)
                                        at_least(pe, xs_ready, at + n - 2)
                                        nc.tensor.matmul(pb[:, b, 0:c1 - c0], kron_pre[:].rearrange("p h i -> p (h i)"),
                                                         dots[:, b, 0:c1 - c0], start=True, stop=True).then_inc(mixed, 1)

                            def back(s, i, j):
                                t, k = 2 * i + j, n_copies[s]
                                at = before(lambda g: n_copies[g], s) + t * k
                                pe.wait_ge(p_ready, s * UT + t + 1)
                                for n, ks in enumerate(copies_of(s)):
                                    b = (j * k + n) % 2
                                    at_least(pe, at_ready, at + n - 1)
                                    for m, kb in enumerate(ks):
                                        rows = dict(key_blocks(s))[kb]
                                        mm = nc.tensor.matmul(pc[0:rows, b, m * P:(m + 1) * P],
                                                              ex[:, j, first_of[kb]:first_of[kb] + rows], mix[:, j, :],
                                                              start=True, stop=True)
                                    mm.then_inc(turned, 1)

                            def weigh(s):
                                pe.wait_ge(at_ready, before(lambda g: n_copies[g], s + 1))
                                at_least(pe, av_done, s)
                                blocks = key_blocks(s)
                                for r in range(PAIRS):
                                    for k, rows in blocks:
                                        for half in range(2):
                                            h = 2 * r + half
                                            mm = nc.tensor.matmul(
                                                po[half * DH1:(half + 1) * DH1, r, :], vn[0:rows, k, h * DH1:(h + 1) * DH1],
                                                aT[0:rows, k, :, h * IL:(h + 1) * IL],
                                                start=(k == 0), stop=(k == blocks[-1][0]))
                                mm.then_inc(av_ready, 1)

                            for j in range(2):
                                front(0, 0, j)
                            for s in range(G):
                                def steady(i):
                                    for j in range(2):
                                        front(s, i + 1, j)
                                    for j in range(2):
                                        back(s, i, j)

                                if s == 0:
                                    for i in range(PQ - 1):
                                        steady(i)
                                else:
                                    with pe.Fori(0, PQ - 1) as i:
                                        steady(i)
                                if s + 1 < G:
                                    for j in range(2):
                                        front(s + 1, 0, j)
                                for j in range(2):
                                    back(s, PQ - 1, j)
                                weigh(s)

                    @block.scalar
                    def _(act):
                        with act.If(again > 0):
                            def front(s, i, j):
                                k, t = n_pieces[s], 2 * i + j
                                at = before(lambda g: n_pieces[g], s) + t * k
                                const = isinstance(i, int)
                                for n, (c0, c1) in enumerate(pieces(s)):
                                    b = (j * k + n) % 2
                                    act.wait_ge(qk_ready, at + n + 1)
                                    at_least(act, mixed, at + n - 1)
                                    nc.scalar.copy(dots[:, b, 0:c1 - c0], pa[:, b, 0:c1 - c0]).then_inc(dots_ready, 1)
                                    if n == 0:
                                        at_least(act, p_ready, (s * PQ + i - 1) * 2)
                                    act.wait_ge(mixed, at + n + 1)
                                    if not const:
                                        act.sem_inc(gate_act, 1)
                                    q = (i % 2) if const else (i % 2)
                                    dst = xs[:, q, j, c0:c1] if const else xs[:, bass.ds(q, 1), j, c0:c1]
                                    nc.scalar.copy(dst, pb[:, b, 0:c1 - c0]).then_inc(xs_ready, 1)

                            def exps(s, i):
                                for j in range(2):
                                    t = s * UT + 2 * i + j
                                    const = isinstance(i, int)
                                    act.wait_ge(negmax, t + 1)
                                    if const and i == 0:
                                        if s > 0:
                                            act.wait_ge(turned, before(lambda g: n_copies[g], s) - n_copies[s - 1] * (1 - j))
                                    else:
                                        act.wait_ge(turned, before(lambda g: n_copies[g], s)
                                                    + (2 * i + j - 1) * n_copies[s])
                                    if not const:
                                        act.sem_inc(gate_act, 1)
                                    q = i % 2
                                    src = xs[:, q, j, 0:width[s]] if const else xs[:, bass.ds(q, 1), j, 0:width[s]]
                                    nc.scalar.activation(ex[:, j, 0:width[s]], src, ACT.Exp,
                                                         bias=sc[:, j, 0:1]).then_inc(ex_ready, 1)

                            def back(s, i, j):
                                t, k = 2 * i + j, n_copies[s]
                                at = before(lambda g: n_copies[g], s) + t * k
                                const = isinstance(i, int)
                                for n, ks in enumerate(copies_of(s)):
                                    b = (j * k + n) % 2
                                    rows = dict(key_blocks(s))[ks[0]]
                                    act.wait_ge(turned, at + n + 1)
                                    if not const:
                                        act.sem_inc(gate_act, 1)
                                    at_u = t if const else bass.ds(t, 1)
                                    src = pc[0:rows, b, 0:len(ks) * P]
                                    dst = (aT[0:rows, ks[0]:ks[-1] + 1, at_u, :])
                                    nc.scalar.copy(dst, src.rearrange("p (k c) -> p k c", c=P)).then_inc(at_ready, 1)

                            def steady(s, i):
                                exps(s, i)
                                for j in range(2):
                                    front(s, i + 1, j)
                                for j in range(2):
                                    back(s, i, j)

                            for j in range(2):
                                front(0, 0, j)
                            for s in range(G):
                                if s == 0:
                                    for i in range(PQ - 1):
                                        steady(s, i)
                                else:
                                    steady(s, 0)
                                    with act.Fori(1, PQ - 1) as i:
                                        steady(s, i)
                                exps(s, PQ - 1)
                                if s + 1 < G:
                                    for j in range(2):
                                        front(s + 1, 0, j)
                                for j in range(2):
                                    back(s, PQ - 1, j)
                                act.wait_ge(av_ready, s + 1)
                                nc.scalar.copy(qT[:, :, s * DH1:(s + 1) * DH1], po[:]).then_inc(av_done, 1)

                    @block.vector
                    def _(dve):
                        with dve.If(again > 0):
                            CHAIN = 2 * (1 + 8 + 7 + 2)

                            def pair(s, i, parity):
                                n = [parity * CHAIN]
                                w = width[s]

                                def do(ins):
                                    n[0] += 1
                                    return ins.then_inc(step, 1)

                                x = [xs[:, parity, j, 0:w] for j in range(2)]
                                u = [wk[:, j, 0:w] for j in range(2)]
                                for j in range(2):
                                    t = 2 * i + j
                                    dve.wait_ge(xs_ready, before(lambda g: n_pieces[g], s) + (t + 1) * n_pieces[s])
                                    at = (UT - 1) * IL - t * IL
                                    m = slide[:, bass.ds(at, DH1)] if not isinstance(at, int) else slide[:, at:at + DH1]
                                    do(nc.vector.tensor_tensor(xs[:, parity, j, w - DH1:w], xs[:, parity, j, w - DH1:w],
                                                               m, ALU.add))
                                for r in range(8):
                                    for j in range(2):
                                        dve.wait_ge(step, n[0] - 1)
                                        do(nc.vector.max(top64[:, j, r, :], x[j] if r == 0 else u[j]))
                                    if r == 0:
                                        for j in range(2):
                                            dve.wait_ge(step, n[0] - 1 + j)
                                            nc.vector.tensor_scalar(sc[:, j, 0:1], top64[:, j, 0, 0:1], -1.0, None,
                                                                    ALU.mult).then_inc(negmax, 1)
                                    if r == 7:
                                        break
                                    for j in range(2):
                                        dve.wait_ge(step, n[0] - 1)
                                        do(nc.vector.match_replace(u[j], top64[:, j, r, :], x[j] if r == 0 else u[j], -BIG))
                                for j in range(2):
                                    dve.wait_ge(ex_ready, s * UT + 2 * i + j + 1)
                                    dve.wait_ge(step, n[0] - 1)
                                    nc.vector.scalar_tensor_tensor(ex[:, j, 0:w], x[j], top64[:, j, 7, 7:8], ex[:, j, 0:w],
                                                                   ALU.is_ge, ALU.mult, accum_out=sc[:, j, 1:2]
                                                                   ).then_inc(step, 1)
                                    n[0] += 1
                                for j in range(2):
                                    dve.wait_ge(step, n[0] - 1)
                                    do(nc.vector.reciprocal(sc[:, j, 2:3], sc[:, j, 1:2]))
                                for j in range(2):
                                    dve.wait_ge(step, n[0] - 1 + j)
                                    nc.vector.tensor_scalar(mix[:, j, :], kron_post[:].rearrange("p h i -> p (h i)"),
                                                            sc[:, j, 2:3], None, ALU.mult).then_inc(p_ready, 1)
                                return n[0]

                            for s in range(G):
                                with dve.Fori(0, PQ // 2) as i2:
                                    dve.sem_clear(step)
                                    pair(s, 2 * i2, 0)
                                    total = pair(s, 2 * i2 + 1, 1)
                                    dve.wait_ge(step, total)

            with ExitStack() as ctx:
                wg = sb("wg", [P, HW], ctx=ctx)
                wo = sb("wo", [P, PAIRS, D], ctx=ctx)
                bgc = sb("bgc", [P, PAIRS], ctx=ctx)
                hs = sb("hs", [P, PAIRS], ctx=ctx)
                sig = sb("sig", [P, 2, N], ctx=ctx)
                res = sb("res", [P, NT, D], ctx=ctx)
                pz = ps("pz", [P, 2, N], ctx)
                py = ps("py", [P, 2, 512], ctx)
                (in_wg, in_g, z_ready, sig_ready, gated, y_ready, s_done, res_ready, out_stored) = fresh(
                    ctx, "in_wg", "in_g", "z_ready", "sig_ready", "gated", "y_ready", "s_done", "res_ready", "out_stored")
                with nc.Block() as block:
                    @block.sync
                    def _(sp):
                        with nc.allow_non_contiguous_dma("a bias and a scale for each channel"):
                            sp.dma_start(wg[:], A["L1_attn_Wg"]).then_inc(in_wg, 16)
                            sp.dma_start(wo[:], A["L1_attn_Wo"].rearrange("(r p) d -> p r d", p=P)).then_inc(in_g, 16)
                            sp.dma_start(bgc[:], A["L1_attn_bg"].rearrange("(r p) -> p r", p=P)).then_inc(in_g, 16)
                            scale = A["L1_attn_head_scale_params"].rearrange("a (r two) b c -> two (a r b c)", two=2)
                            for two in range(2):
                                sp.dma_start(hs[two * DH1:(two + 1) * DH1, :], scale[two].partition_broadcast(DH1)
                                             ).then_inc(in_g, 16)
                        for q in range(2):
                            sp.wait_ge(res_ready, q + 1)
                            sp.dma_start(out.rearrange("b (t p) d -> p (b t) d", p=P)
                                         [:, bass.ds(batch * NT + 4 * q, 4), :], res[:, 4 * q:4 * q + 4, :]
                                         ).then_inc(out_stored, 16)
                        sp.wait_ge(out_stored, 32)

                    @block.tensor
                    def _(pe):
                        pe.wait_ge(in_wg, 16)
                        for r in range(PAIRS):
                            if r >= 2:
                                pe.wait_ge(sig_ready, r - 1)
                            for c in range(2):
                                mm = nc.tensor.matmul(pz[:, r % 2, c * 512:(c + 1) * 512], wg[:, r * P:(r + 1) * P],
                                                      xnT[:, MEM + c * 512:MEM + (c + 1) * 512], start=True, stop=True)
                            mm.then_inc(z_ready, 1)
                        pe.wait_ge(in_g, 16 * 4)
                        pe.wait_ge(gated, PAIRS)
                        for q in range(2):
                            for t in range(4 * q, 4 * q + 4):
                                for r in range(PAIRS):
                                    mm = nc.tensor.matmul(py[:, q, (t % 4) * P:(t % 4 + 1) * P], qT[:, r, t * P:(t + 1) * P],
                                                          wo[:, r, :], start=(r == 0), stop=(r == PAIRS - 1))
                            mm.then_inc(y_ready, 1)

                    @block.scalar
                    def _(act):
                        act.wait_ge(in_g, 16 * 4)
                        for r in range(PAIRS):
                            act.wait_ge(z_ready, r + 1)
                            if r >= 2:
                                act.wait_ge(gated, r - 1)
                            nc.scalar.activation(sig[:, r % 2, :], pz[:, r % 2, :], ACT.Sigmoid, bias=bgc[:, r:r + 1]
                                                 ).then_inc(sig_ready, 1)

                    @block.vector
                    def _(dve):
                        for r in range(PAIRS):
                            dve.wait_ge(sig_ready, r + 1)
                            nc.vector.scalar_tensor_tensor(qT[:, r, :], sig[:, r % 2, :], hs[:, r:r + 1], qT[:, r, :],
                                                           ALU.mult, ALU.mult).then_inc(gated, 1)
                        for q in range(2):
                            half = slice(4 * q, 4 * q + 4)
                            dve.wait_ge(y_ready, q + 1)
                            nc.vector.tensor_tensor(res[:, half, :], py[:, q, :].rearrange("p (t d) -> p t d", d=D),
                                                    g1[:, half, :], ALU.mult).then_inc(s_done, 1)
                            dve.wait_ge(s_done, q + 1)
                            nc.vector.tensor_tensor(res[:, half, :], res[:, half, :], xb[:, half, :],
                                                    ALU.add).then_inc(res_ready, 1)


def kernel(**inputs):
    import numpy as np
    import concourse.bacc as bacc
    from concourse.bass_utils import run_bass_kernel_spmd

    nc = bacc.Bacc("TRN2", target_bir_lowering=False, num_devices=1)
    arrays = {f"in_{name}": np.ascontiguousarray(a) for name, a in inputs.items()}
    A = {name: nc.dram_tensor(f"in_{name}", a.shape, mybir.dt.from_np(a.dtype), kind="ExternalInput").ap()
         for name, a in ((n, arrays[f"in_{n}"]) for n in inputs)}
    out = nc.dram_tensor("out_dram", inputs["L0_attn_x"].shape, F32, kind="ExternalOutput").ap()
    program(nc, A, out)
    got = run_bass_kernel_spmd(nc, [arrays], core_ids=[0])
    return got.results[0]["out_dram"]
```
